# Optimizing a Trainium2 kernel written in Bass

```python
import numpy as np
import jax
import jax.numpy as jnp

def _softmax(x, axis=-1):
    return jax.nn.softmax(x, axis=axis)

def _gelu(x):
    return jax.nn.gelu(x, approximate=True)

def _silu(x):
    return jax.nn.silu(x)

def _sigmoid(x):
    return jax.nn.sigmoid(x)

def _layernorm(x, axis=-1, eps=1e-05):
    m = jnp.mean(x, axis=axis, keepdims=True)
    v = jnp.var(x, axis=axis, keepdims=True)
    return (x - m) / jnp.sqrt(v + eps)

def _scatter_add(tgt, idx, src, axis=0):
    return tgt.at[idx].add(src)

def _segment_sum(src, seg, n):
    return jax.ops.segment_sum(src, seg, n)
kernel_name = 'mk_lm_tower_d2_tok_ids1024_r4_939beb'

def setup_inputs(seed: int=0):
    np.random.seed(seed)
    _w = jnp.asarray

    def _rec_inputs():
        import jax
        import jax.numpy as jnp
        _rk = jax.random.key(seed)
        x = jax.random.randint(jax.random.fold_in(_rk, 1), (16, 128), 0, 30521, jnp.int32)
        mask_BS_i1_0 = jnp.where(jnp.ones((16, 128), dtype=bool), 1, 0).astype(jnp.int32)
        return (x, mask_BS_i1_0)
    x, mask_BS_i1_0 = _rec_inputs()

    def _L0_tok_setup():
        import jax, jax.numpy as jnp
        import numpy as np
        VOCAB = 30522
        HIDDEN = 256
        MAX_POS = 128
        TYPES = 2
        EPS = 1e-12
        key = jax.random.key(seed)
        k1, k2, k3, k4, k5 = jax.random.split(key, 5)
        B, S = (32, 128)
        input_ids = jax.random.randint(k1, (B, S), 0, VOCAB, dtype=jnp.int64 if jax.config.jax_enable_x64 else jnp.int32)
        token_type_ids = jax.random.randint(k2, (B, S), 0, TYPES, dtype=input_ids.dtype)
        word_emb = jax.random.normal(k3, (VOCAB, HIDDEN), dtype=jnp.float32) * 0.02
        word_emb = word_emb.at[0].set(0.0)
        pos_emb = jax.random.normal(k4, (MAX_POS, HIDDEN), dtype=jnp.float32) * 0.02
        type_emb = jax.random.normal(k5, (TYPES, HIDDEN), dtype=jnp.float32) * 0.02
        gamma = jnp.ones((HIDDEN,), dtype=jnp.float32)
        beta = jnp.zeros((HIDDEN,), dtype=jnp.float32)
        return {'input_ids': input_ids, 'token_type_ids': token_type_ids, 'word_emb': word_emb, 'pos_emb': pos_emb, 'type_emb': type_emb, 'gamma': gamma, 'beta': beta}
    _L0_tok_all = _L0_tok_setup()
    _L0_tok_in = {k: v for k, v in _L0_tok_all.items() if k in ('word_emb', 'pos_emb', 'type_emb', 'gamma', 'beta')}
    del _L0_tok_all

    def _L0_attn_setup():
        import jax, jax.numpy as jnp
        import numpy as np
        DIM = 256
        key = jax.random.key(seed)
        k1, k2, k3, k4 = jax.random.split(key, 4)
        x = jax.random.normal(k1, (4, 512, DIM), dtype=jnp.float32)
        wk = jax.random.normal(k2, (DIM, DIM), dtype=jnp.float32) * 0.02
        wq = jax.random.normal(k3, (DIM, DIM), dtype=jnp.float32) * 0.02
        wv = jax.random.normal(k4, (DIM, DIM), dtype=jnp.float32) * 0.02
        return {'x': x, 'wk': wk, 'wq': wq, 'wv': wv}
    _L0_attn_all = _L0_attn_setup()
    _L0_attn_in = {k: v for k, v in _L0_attn_all.items() if k in ('wk', 'wq', 'wv')}
    del _L0_attn_all

    def _L0_ffn_setup():
        import jax, jax.numpy as jnp
        import numpy as np
        D = 256
        H = 16
        HD = D // H
        L = 64
        E = 8
        B, T = (4, 512)
        EPS = 1e-06

        def _glorot(k, shape):
            fan_in, fan_out = (shape[-2], shape[-1])
            lim = np.sqrt(6.0 / (fan_in + fan_out)).astype(np.float32)
            return jax.random.uniform(k, shape, jnp.float32, -lim, lim)

        def _rmsnorm(x, gamma):
            return gamma * x * jax.lax.rsqrt(jnp.mean(x * x, axis=-1, keepdims=True) + EPS)
        key = jax.random.key(seed)
        ks = jax.random.split(key, 8)
        return {'x': jax.random.normal(ks[0], (B, T, D), jnp.float32), 'gamma1': jnp.ones((D,), jnp.float32), 'Wq': _glorot(ks[1], (D, D)), 'bq': jnp.zeros((D,), jnp.float32), 'Wdown': _glorot(ks[2], (D, L)), 'bdown': jnp.zeros((L,), jnp.float32), 'Wup': _glorot(ks[3], (L, 2 * D)), 'bup': jnp.zeros((2 * D,), jnp.float32), 'Wo': _glorot(ks[4], (D, D)), 'bo': jnp.zeros((D,), jnp.float32), 'gamma2': jnp.ones((D,), jnp.float32), 'Wg': _glorot(ks[5], (D, E)), 'bg': jnp.zeros((E,), jnp.float32), 'We': _glorot(ks[6], (E, D, D))}
    _L0_ffn_all = _L0_ffn_setup()
    _L0_ffn_in = {k: v for k, v in _L0_ffn_all.items() if k in ('gamma1', 'Wq', 'bq', 'Wdown', 'bdown', 'Wup', 'bup', 'Wo', 'bo', 'gamma2', 'Wg', 'bg', 'We')}
    del _L0_ffn_all

    def _L1_attn_setup():
        import jax, jax.numpy as jnp
        import numpy as np
        MODEL_DIM = 256
        NUM_HEADS = 16
        HEAD_DIM = MODEL_DIM // NUM_HEADS
        ROPE_PERIOD = 10000.0

        def _rope_cos_sin(seq_len, dim, dtype):
            inv_freq = 1.0 / ROPE_PERIOD ** (jnp.arange(0, dim, 2, dtype=jnp.float32) / dim)
            t = jnp.arange(seq_len, dtype=jnp.float32)
            freqs = jnp.outer(t, inv_freq)
            emb = jnp.concatenate([freqs, freqs], axis=-1)
            return (jnp.cos(emb).astype(dtype), jnp.sin(emb).astype(dtype))

        def _rope_embed(x):
            S, D = (x.shape[-2], x.shape[-1])
            cos, sin = _rope_cos_sin(S, D, x.dtype)
            x1 = x[..., :D // 2]
            x2 = x[..., D // 2:]
            rotated = jnp.concatenate([-x2, x1], axis=-1)
            return x * cos + rotated * sin
        key = jax.random.key(seed)
        kx, kq, kk, kv, ko = jax.random.split(key, 5)
        std = 0.02
        return {'x': jax.random.normal(kx, (2, 512, MODEL_DIM), dtype=jnp.float32), 'Wq': std * jax.random.normal(kq, (MODEL_DIM, MODEL_DIM), dtype=jnp.float32), 'Wk': std * jax.random.normal(kk, (MODEL_DIM, MODEL_DIM), dtype=jnp.float32), 'Wv': std * jax.random.normal(kv, (MODEL_DIM, MODEL_DIM), dtype=jnp.float32), 'Wo': std * jax.random.normal(ko, (MODEL_DIM, MODEL_DIM), dtype=jnp.float32)}
    _L1_attn_all = _L1_attn_setup()
    _L1_attn_in = {k: v for k, v in _L1_attn_all.items() if k in ('Wq', 'Wk', 'Wv', 'Wo')}
    del _L1_attn_all

    def _L1_ffn_setup():
        import jax, jax.numpy as jnp
        import numpy as np
        S, B, H, I, E = (128, 2, 256, 704, 8)
        key = jax.random.key(seed)
        ks = jax.random.split(key, 5)
        return {'hidden_states': jax.random.normal(ks[0], (S, B, H), dtype=jnp.float32), 'router_w': jax.random.normal(ks[1], (E, H), dtype=jnp.float32) * 0.02, 'gate_w': jax.random.normal(ks[2], (E, I, H), dtype=jnp.float32) * 0.02, 'up_w': jax.random.normal(ks[3], (E, I, H), dtype=jnp.float32) * 0.02, 'down_w': jax.random.normal(ks[4], (E, H, I), dtype=jnp.float32) * 0.02}
    _L1_ffn_all = _L1_ffn_setup()
    _L1_ffn_in = {k: v for k, v in _L1_ffn_all.items() if k in ('router_w', 'gate_w', 'up_w', 'down_w')}
    del _L1_ffn_all
    return {'x': x, 'mask_BS_i1_0': mask_BS_i1_0, 'L0_tok_word_emb': _L0_tok_in['word_emb'], 'L0_tok_pos_emb': _L0_tok_in['pos_emb'], 'L0_tok_type_emb': _L0_tok_in['type_emb'], 'L0_tok_gamma': _L0_tok_in['gamma'], 'L0_tok_beta': _L0_tok_in['beta'], 'L0_attn_wk': _L0_attn_in['wk'], 'L0_attn_wq': _L0_attn_in['wq'], 'L0_attn_wv': _L0_attn_in['wv'], 'L0_ffn_gamma1': _L0_ffn_in['gamma1'], 'L0_ffn_Wq': _L0_ffn_in['Wq'], 'L0_ffn_bq': _L0_ffn_in['bq'], 'L0_ffn_Wdown': _L0_ffn_in['Wdown'], 'L0_ffn_bdown': _L0_ffn_in['bdown'], 'L0_ffn_Wup': _L0_ffn_in['Wup'], 'L0_ffn_bup': _L0_ffn_in['bup'], 'L0_ffn_Wo': _L0_ffn_in['Wo'], 'L0_ffn_bo': _L0_ffn_in['bo'], 'L0_ffn_gamma2': _L0_ffn_in['gamma2'], 'L0_ffn_Wg': _L0_ffn_in['Wg'], 'L0_ffn_bg': _L0_ffn_in['bg'], 'L0_ffn_We': _L0_ffn_in['We'], 'L1_attn_Wq': _L1_attn_in['Wq'], 'L1_attn_Wk': _L1_attn_in['Wk'], 'L1_attn_Wv': _L1_attn_in['Wv'], 'L1_attn_Wo': _L1_attn_in['Wo'], 'L1_ffn_router_w': _L1_ffn_in['router_w'], 'L1_ffn_gate_w': _L1_ffn_in['gate_w'], 'L1_ffn_up_w': _L1_ffn_in['up_w'], 'L1_ffn_down_w': _L1_ffn_in['down_w']}

def reference(x, mask_BS_i1_0, L0_tok_word_emb, L0_tok_pos_emb, L0_tok_type_emb, L0_tok_gamma, L0_tok_beta, L0_attn_wk, L0_attn_wq, L0_attn_wv, L0_ffn_gamma1, L0_ffn_Wq, L0_ffn_bq, L0_ffn_Wdown, L0_ffn_bdown, L0_ffn_Wup, L0_ffn_bup, L0_ffn_Wo, L0_ffn_bo, L0_ffn_gamma2, L0_ffn_Wg, L0_ffn_bg, L0_ffn_We, L1_attn_Wq, L1_attn_Wk, L1_attn_Wv, L1_attn_Wo, L1_ffn_router_w, L1_ffn_gate_w, L1_ffn_up_w, L1_ffn_down_w):
    import jax
    import jax.numpy as jnp

    def _L0_tok_ref(input_ids, token_type_ids, word_emb, pos_emb, type_emb, gamma, beta):
        import jax, jax.numpy as jnp
        import numpy as np
        VOCAB = 30522
        HIDDEN = 256
        MAX_POS = 128
        TYPES = 2
        EPS = 1e-12
        B, S = input_ids.shape
        x = word_emb[input_ids]
        x = x + pos_emb[jnp.arange(S)][None, :, :]
        x = x + type_emb[token_type_ids]
        mean = jnp.mean(x, axis=-1, keepdims=True)
        var = jnp.mean(jnp.square(x - mean), axis=-1, keepdims=True)
        x = (x - mean) * jax.lax.rsqrt(var + EPS)
        x = x * gamma + beta
        return x

    def _L0_attn_ref(x, wk, wq, wv):
        import jax, jax.numpy as jnp
        import numpy as np
        DIM = 256
        B, N, d = x.shape
        scale = N ** (-0.5)
        wv_stoch = (jax.nn.softmax(wv, axis=0) * (1.0 / d)).T
        query = x @ wq
        key_t = jnp.swapaxes(x @ wk, -1, -2)
        value = x @ wv_stoch
        scores = jnp.einsum('bnd,bdm->bnm', query, key_t) * scale
        attn = jax.nn.softmax(scores, axis=1) - jnp.eye(N, dtype=x.dtype)
        return attn @ value

    def _L0_ffn_ref(x, gamma1, Wq, bq, Wdown, bdown, Wup, bup, Wo, bo, gamma2, Wg, bg, We):
        import jax, jax.numpy as jnp
        import numpy as np
        D = 256
        H = 16
        HD = D // H
        L = 64
        E = 8
        B, T = (4, 512)
        EPS = 1e-06

        def _glorot(k, shape):
            fan_in, fan_out = (shape[-2], shape[-1])
            lim = np.sqrt(6.0 / (fan_in + fan_out)).astype(np.float32)
            return jax.random.uniform(k, shape, jnp.float32, -lim, lim)

        def _rmsnorm(x, gamma):
            return gamma * x * jax.lax.rsqrt(jnp.mean(x * x, axis=-1, keepdims=True) + EPS)
        b, t = (x.shape[0], x.shape[1])
        h = _rmsnorm(x, gamma1)
        q = (h @ Wq + bq).reshape(b, t, H, HD)
        kv = ((h @ Wdown + bdown) @ Wup + bup).reshape(b, t, H, 2 * HD)
        k, v = jnp.split(kv, 2, axis=-1)
        att = jnp.einsum('bthd,btgd->bthg', q, k) / np.sqrt(HD).astype(np.float32)
        att = jax.nn.softmax(att, axis=-1)
        out = jnp.einsum('bthg,btgd->bthd', att, v).reshape(b, t, D)
        x = x + (out @ Wo + bo)
        h2 = _rmsnorm(x, gamma2)
        gate = jax.nn.softmax(h2 @ Wg + bg, axis=-1)
        combined = jnp.einsum('btd,edf,bte->btf', h2, We, gate)
        return x + combined

    def _L1_attn_ref(x, Wq, Wk, Wv, Wo):
        import jax, jax.numpy as jnp
        import numpy as np
        MODEL_DIM = 256
        NUM_HEADS = 16
        HEAD_DIM = MODEL_DIM // NUM_HEADS
        ROPE_PERIOD = 10000.0

        def _rope_cos_sin(seq_len, dim, dtype):
            inv_freq = 1.0 / ROPE_PERIOD ** (jnp.arange(0, dim, 2, dtype=jnp.float32) / dim)
            t = jnp.arange(seq_len, dtype=jnp.float32)
            freqs = jnp.outer(t, inv_freq)
            emb = jnp.concatenate([freqs, freqs], axis=-1)
            return (jnp.cos(emb).astype(dtype), jnp.sin(emb).astype(dtype))

        def _rope_embed(x):
            S, D = (x.shape[-2], x.shape[-1])
            cos, sin = _rope_cos_sin(S, D, x.dtype)
            x1 = x[..., :D // 2]
            x2 = x[..., D // 2:]
            rotated = jnp.concatenate([-x2, x1], axis=-1)
            return x * cos + rotated * sin
        B, S, Dm = x.shape
        H, Dh = (NUM_HEADS, HEAD_DIM)
        q = (x @ Wq.T).reshape(B, S, H, Dh).transpose(0, 2, 1, 3)
        k = (x @ Wk.T).reshape(B, S, H, Dh).transpose(0, 2, 1, 3)
        v = (x @ Wv.T).reshape(B, S, H, Dh).transpose(0, 2, 1, 3)
        q = _rope_embed(q)
        k = _rope_embed(k)
        scores = jnp.einsum('bhqd,bhkd->bhqk', q, k) / jnp.sqrt(jnp.asarray(Dh, x.dtype))
        neg_inf = jnp.finfo(x.dtype).min
        causal = jnp.triu(jnp.full((S, S), neg_inf, dtype=x.dtype), k=1)
        scores = scores + causal
        attn = jax.nn.softmax(scores, axis=-1)
        out = jnp.einsum('bhqk,bhkd->bhqd', attn, v)
        out = out.transpose(0, 2, 1, 3).reshape(B, S, Dm)
        return out @ Wo.T

    def _L1_ffn_ref(hidden_states, router_w, gate_w, up_w, down_w):
        import jax, jax.numpy as jnp
        import numpy as np
        S, B, H, I, E = (128, 2, 256, 704, 8)
        router_logits = jnp.einsum('sbh,eh->sbe', hidden_states, router_w)
        routing_indices = jnp.argmax(router_logits, axis=-1)
        out = jnp.zeros_like(hidden_states)
        for e in range(E):
            mask = (routing_indices == e)[..., None]
            xe = jnp.where(mask, hidden_states, 0.0)
            g = jnp.einsum('sbh,ih->sbi', xe, gate_w[e])
            u = jnp.einsum('sbh,ih->sbi', xe, up_w[e])
            ye = jnp.einsum('sbi,hi->sbh', jax.nn.silu(g) * u, down_w[e])
            out = out + jnp.where(mask, ye, 0.0)
        return out
    h = _L0_tok_ref(x, mask_BS_i1_0, L0_tok_word_emb, L0_tok_pos_emb, L0_tok_type_emb, L0_tok_gamma, L0_tok_beta)
    h = h + _L0_attn_ref(_layernorm(h, axis=-1), L0_attn_wk, L0_attn_wq, L0_attn_wv)
    h = h + _L0_ffn_ref(_layernorm(h, axis=-1), L0_ffn_gamma1, L0_ffn_Wq, L0_ffn_bq, L0_ffn_Wdown, L0_ffn_bdown, L0_ffn_Wup, L0_ffn_bup, L0_ffn_Wo, L0_ffn_bo, L0_ffn_gamma2, L0_ffn_Wg, L0_ffn_bg, L0_ffn_We)
    h = h + _L1_attn_ref(_layernorm(h, axis=-1), L1_attn_Wq, L1_attn_Wk, L1_attn_Wv, L1_attn_Wo)
    h = h + _L1_ffn_ref(_layernorm(h, axis=-1), L1_ffn_router_w, L1_ffn_gate_w, L1_ffn_up_w, L1_ffn_down_w)
    return h

_drawn_inputs = setup_inputs


def setup_inputs(seed=0):
    import zlib

    import numpy as np

    out = dict(_drawn_inputs(seed))
    spreads = {'L0_tok_gamma': (1.0, 0.2),
     'L0_tok_beta': (0.0, 0.1),
     'L0_ffn_gamma1': (1.0, 0.2),
     'L0_ffn_bq': (0.0, 0.8),
     'L0_ffn_bdown': (0.0, 0.8),
     'L0_ffn_bup': (0.0, 0.386),
     'L0_ffn_bo': (0.0, 0.1),
     'L0_ffn_gamma2': (1.0, 0.2),
     'L0_ffn_bg': (0.0, 0.558)}
    factors = {'L0_attn_wk': 200.0,
     'L0_attn_wq': 200.0,
     'L0_attn_wv': 200.0,
     'L1_attn_Wq': 8.0,
     'L1_attn_Wk': 8.0,
     'L1_ffn_router_w': 4.581,
     'L1_ffn_gate_w': 4.279,
     'L1_ffn_up_w': 4.285,
     'L1_ffn_down_w': 4.222}
    for name, (base, spread) in spreads.items():
        noise = np.random.default_rng([zlib.crc32(name.encode()), seed]).standard_normal(out[name].shape)
        drawn = base * np.exp(spread * noise) if base else spread * noise
        out[name] = jnp.asarray(drawn.astype(out[name].dtype))
    for name, factor in factors.items():
        out[name] = (out[name] * factor).astype(out[name].dtype)
    return out
```

```python
from contextlib import ExitStack

import numpy as np

import concourse.bass as bass
from concourse import mybir

F32 = mybir.dt.float32
F32R = mybir.dt.float32r
BF16 = mybir.dt.bfloat16
I32 = mybir.dt.int32
U32 = mybir.dt.uint32
ALU = mybir.AluOpType
ACT = mybir.ActivationFunctionType
AX = mybir.AxisListType

P = 128
B = 16
D = 256
KD = D // P
H = 16
HD = D // H
NB = H // 2
PART = 3 * HD
AUG = PART + 2
LAT = 64
E = 8
I = 704
IH = I // 2
KI = (I + P - 1) // P
IR = I - (KI - 1) * P
GU = KD * 2 * I
WE = GU + KI * D
NJ = B + E - 1
HP = 5
NEG = -3.0e38
SCALE0 = float(P) ** -0.5
SCALEH = float(HD) ** -0.5
FAR = 8192.0

SEMAPHORES = (
    "small_in ids_in w0_in wf_in w1_in rows_in experts_in "
    "p_set masks ident_b prep wa_ps wa wv_mx wv_ex wv_ri wv_s wf_s "
    "n0_st n0_ag n0_ep n0_rs n1_st n1_ag n1_ep n1_rs n2_ag n2_ep n2_rs "
    "a_x a_xt a_ng a_h a_xn a_T a_xT a_u a_v a_uT a_vs a_S a_mr a_mx a_E a_ri a_vn a_O a_hv a_done "
    "b_x2 b_xn b_T b_xT b_q b_c b_cT b_kv b_kf b_qf b_vf "
    "g_qk_mul g_S g_max g_sub g_exp g_sum g_ri g_pv_pool g_pv_dve g_O g_o g_oT g_oTs g_Wo g_upd "
    "c_xn c_T c_xT c_lg c_lb c_mx c_ex c_ri c_gt c_exp c_es c_sum c_acc "
    "d_xn d_T d_xT d_qk d_v d_rot d_qf d_vf "
    "e_xn e_T e_xT e_lg e_lgs e_hout e_xout0 e_xout1 "
    "h_hi h_dup h_lo h_padT h_qkT h_S1 h_max h_nh h_nl h_nT h_nTs h_aug h_S2 h_exp h_va h_AV h_OTs "
    "h_OTT h_ri h_o h_oT h_oTs h_Wo h_upd "
    "r_pe r_dve r_hots r_tables "
    "f_gi f_xin0 f_xin1 f_T f_xT f_gate f_up f_silu f_hm f_Ta f_Tb f_hTa f_hTb f_down f_hi f_hin0 f_hin1 f_y "
    "f_si f_out0 f_out1"
).split()

NORMS = {"a0": (0, 0), "b0": (0, B), "d0": (0, 2 * B), "a1": (1, 0), "b1": (1, B), "e1": (1, 2 * B), "c0": (2, 0)}
TAKEN = {"a0": 0, "b0": B, "d0": 2 * B, "a1": 0, "e1": B}


def rows(ap, k):
    return ap.rearrange("(k p) n -> p k n", k=k)


def build(nc, dr):
    with ExitStack() as ctx:
        program(nc, dr, ctx)


def program(nc, dr, ctx):
    def sb(name, shape, dt=F32):
        return ctx.enter_context(nc.sbuf_tensor(name, shape, dt))

    s = {name: ctx.enter_context(nc.semaphore(name)) for name in SEMAPHORES}

    def due(n):
        return not isinstance(n, int) or n > 0

    def ready(eng, n):
        return n if isinstance(n, int) else eng.to_reg(n)

    W = sb("W", [P, E, WE])
    h = sb("h", [P, B, D])
    v_all = sb("v_all", [P, B * D])
    pad = sb("pad", [P, 2, H, 64], F32R)
    qT = [sb(f"qT{u}", [P, NB, P], F32R) for u in range(2)]
    kT = [[sb(f"kT{u}_{f}", [P, NB, P], F32R) for f in range(2)] for u in range(2)]
    nms = sb("nms", [P, P], F32R)
    nmT = sb("nmT", [32, P], F32R)
    ident = sb("ident", [P, P])
    ident_b = sb("ident_b", [P, P], BF16)
    mask_qk = sb("mask_qk", [P, P], BF16)
    mask_kq = sb("mask_kq", [P, P], BF16)
    before = sb("before", [P, P], BF16)
    ones_b = sb("ones_b", [P, P], BF16)
    neghalf = sb("neghalf", [P, 1])
    w_router = sb("w_router", [P, KD, E])
    stat = [sb(f"stat{u}", [P, 6]) for u in range(3)]
    mv = [[sb(f"mv{n}_{u}", [P, 2]) for u in range(2)] for n in range(3)]
    rs = [[sb(f"rs{n}_{u}", [P, 2]) for u in range(2)] for n in range(3)]
    nmax = sb("nmax", [P, H])
    rinv = sb("rinv", [P, H])
    LG = sb("LG", [P, B, E])
    idx_i = sb("idx_i", [P, 2, NJ], I32)
    texp_i = sb("texp_i", [P, NJ], I32)
    gi = [sb(f"gi{u}", [P, 1], I32) for u in range(2)]
    hi_ = [sb(f"hi{u}", [P, 1], I32) for u in range(2)]
    si = [sb(f"si{u}", [P, 1], I32) for u in range(2)]
    ids = sb("ids", [P, B], I32)
    typ_i = sb("typ_i", [P, B], I32)
    cst = sb("cst", [P, E + 2 * B + NJ + P])
    v_tiles = v_all[:].rearrange("p (b d) -> p b d", b=B)
    t01 = v_all[:, 0:2 * D].rearrange("p (a d) -> p a d", a=2)

    first = {0: 0, 2: 0, 5: 0}

    def carve(e0, shape, parts=P):
        n = int(np.prod(shape))
        at = first[e0]
        first[e0] = at + n
        count = 3 if e0 else 2
        assert first[e0] <= count * WE, first
        flat = W[:, e0:e0 + count, :].rearrange("p e w -> p (e w)")[0:parts, at:at + n]
        if len(shape) == 2:
            flat = flat.rearrange("p (a b) -> p a b", a=shape[0])
        if len(shape) == 3:
            flat = flat.rearrange("p (a b c) -> p a b c", a=shape[0], b=shape[1])
        return flat

    qk = carve(0, (H * H * HD,))
    pv = carve(0, (H * H * HD,))
    rsum = [carve(0, (H,)) for _ in range(2)]
    hmax = carve(0, (H,))
    w_e = carve(2, (KD, E * D))
    x2 = carve(2, (B, D))
    wqT = carve(2, (KD, D))
    wkT = carve(2, (KD, D))
    w_a = carve(2, (KD, D))
    w_vs = carve(2, (KD, D))
    w_q = carve(2, (KD, D))
    w_down = carve(2, (KD, LAT))
    w_up = carve(2, (2 * D,), LAT)
    w_o0 = carve(2, (KD, D))
    w_g = carve(2, (KD, E))
    col = carve(2, (8,))
    b_g = carve(2, (E,))
    w_qk1 = carve(5, (KD, 2 * D))
    w_v1 = carve(5, (KD, D))
    w_o1 = carve(5, (KD, D))
    pos_t = carve(5, (D,))
    dtype_ = carve(5, (D,))
    gam = carve(5, (D,))
    bet = carve(5, (D,))
    b_q = carve(2, (D,))
    b_up = carve(2, (2 * D,))
    b_o = carve(2, (D,))
    cosb = carve(5, (HD,))
    sinb = carve(5, (HD,))
    typ = carve(5, (B,))
    wv_small = carve(5, (8,))
    n0 = carve(5, (D,))
    xn = [carve(5, (D,)) for _ in range(2)]
    xT = [carve(5, (KD, P)) for _ in range(2)]
    PT = carve(5, (H, P))
    ots = carve(5, (4 * P,))
    o_sb = carve(5, (D,))
    oT = carve(5, (KD, P))
    vaug = [carve(5, (H, 32)) for _ in range(2)]
    mark = first[5]
    cT = carve(5, (P,), LAT)
    qkf = [carve(5, (2, H, HD)) for _ in range(2)]
    t1 = carve(5, (2 * H, HD))
    t2 = carve(5, (2 * H, HD))
    first[5] = mark
    uT = [carve(5, (KD, P)) for _ in range(2)]
    va_ = [carve(5, (D,)) for _ in range(2)]
    ET = [carve(5, (P,)) for _ in range(2)]
    vn = carve(5, (D,))
    sm = [carve(5, (4,)) for _ in range(2)]
    first[5] = mark + P + 2 * 2 * H * HD
    sc = [carve(5, (H, H)) for _ in range(2)]
    gate = [carve(5, (E,)) for _ in range(2)]
    gsum = [carve(5, (2,)) for _ in range(2)]
    gmax = carve(5, (2,))
    glog = carve(5, (E,))
    es = PT.rearrange("p h t -> p (h t)").rearrange("p (e d) -> p e d", e=E)

    first[5] = max(first[5], mark + 3 * 512 * 2 + P)
    en = [carve(5, (D,)) for _ in range(2)]
    eT = [carve(5, (KD, P)) for _ in range(2)]

    free = [0]

    def table(shape, dt=F32):
        n = int(np.prod(shape))
        lo, free[0] = free[0], free[0] + (n + 1) // 2 * (1 if dt == BF16 else 2)
        lo, hi = lo, free[0]
        flat = v_all[:, lo:lo + n] if dt == F32 else v_all[:, lo:hi].bitcast(dt)[:, 0:n]
        assert hi <= B * D
        return flat.rearrange("p (a b) -> p a b", a=shape[0]) if len(shape) == 2 else \
            flat.rearrange("p (a b c) -> p a b c", a=shape[0], b=shape[1])

    r_hot = table((B, E))
    r_hot_b = table((B, E), BF16)
    r_tmp = table((B, E))
    r_max = table((1, B))[:, 0, :]
    r_n = table((1, E))[:, 0, :]
    r_ci = table((1, E))[:, 0, :]
    r_base = table((1, E))[:, 0, :]
    r_slot = table((1, B))[:, 0, :]
    r_slot_i = table((1, B), I32)[:, 0, :]
    r_a_i = table((1, B), I32)[:, 0, :]
    r_b_i = table((1, B), I32)[:, 0, :]
    r_a = table((1, B))[:, 0, :]
    r_b = table((1, B))[:, 0, :]
    r_cmp = table((E, B))
    r_te = table((NJ, E))
    r_tile = table((1, NJ))[:, 0, :]
    r_id = table((1, NJ))[:, 0, :]
    r_far = table((1, NJ))[:, 0, :]
    r_idg = table((1, NJ))[:, 0, :]
    r_hot_a = table((B, NJ))
    r_hot_c = table((B, P))
    sg = v_all[:, 0:I]
    hm = [v_all[:, I * (1 + u):I * (2 + u)] for u in range(2)]
    late = pad[:].rearrange("p a h c -> p (a h c)").bitcast(F32)
    gx = [late[:, D * u:D * (u + 1)] for u in range(2)]
    xsT = [late[:, D * (2 + u):D * (3 + u)].rearrange("p (k t) -> p k t", k=KD) for u in range(2)]
    hT = [v_all[:, 3 * I:3 * I + KI * P].rearrange("p (k t) -> p k t", k=KI),
          late[:, 4 * D:4 * D + KI * P].rearrange("p (k t) -> p k t", k=KI)]

    lo = 3 * I + KI * P
    gh = [v_all[:, lo + D * u:lo + D * (u + 1)] for u in range(2)]
    yo = [v_all[:, lo + D * (2 + u):lo + D * (3 + u)] for u in range(2)]

    PS = ctx.enter_context(nc.psum_tensor("PS", [P, 8, 512], F32))
    b0, b1, b2, b3, b4, b5, b6, b7 = (PS[:, n, :] for n in range(8))

    h_dram = nc.dram_tensor("h_rows", [B * P, D], F32).ap()
    xn_dram = nc.dram_tensor("xn_rows", [B * P, D], F32).ap()
    out = dr["out"]

    block = ctx.enter_context(nc.Block())

    def skewed(eng, step, n, depth):
        head = depth + 2 - depth % 2
        tail = head + (n - head) // 2 * 2
        for i in range(head):
            step(i, i % 2)
        with eng.Fori(head // 2, tail // 2) as m:
            step(2 * m, 0)
            step(2 * m + 1, 1)
        for i in range(tail, n + depth - 1):
            step(i, i % 2)

    def at(i, k, n=B):
        if isinstance(i, int):
            return i - k if 0 <= i - k < n else None
        return i - k if k else i

    def done(i, k):
        return min(max(i - k + 1, 0), B) if isinstance(i, int) else i - k + 1

    def tile(x, t):
        if isinstance(t, int):
            return x[:, t]
        return x[:, bass.ds(t, 1)].rearrange("p a d -> p (a d)")

    def over_heads(ap):
        return ap.rearrange("p (h d) -> p h d", h=H)

    def heads3(x):
        return x.rearrange("p (h a b) -> p h a b", h=H, a=H)

    def over_keys(p_):
        return p_.unsqueeze(2).to_broadcast([P, p_.shape[1], HD, H])

    def over_queries(v, n):
        return v.rearrange("p (g d) -> p d g", g=H).unsqueeze(1).to_broadcast([P, n, HD, H])

    o_heads = over_heads(o_sb)

    def qk_out(eng, t, u, r, half=None):
        eng.wait_ge(s["h_padT"], 4 * t + r + 1)
        read = 4 * (t - 2) + 3 + r % 2
        if due(read):
            eng.wait_ge(s["h_S2"], read)
        rows_, to = (slice(0, P), qT[u]) if half is None else (slice(64 * half, 64 * half + 64), kT[u][half])
        dst = to[rows_, 4 * (r % 2):4 * (r % 2) + 4, :].rearrange("p b t -> p (b t)")
        if eng is nc.scalar:
            nc.scalar.activation(dst, b0[rows_], ACT.Copy).then_inc(s["h_qkT"], 1)
        else:
            nc.vector.tensor_copy(dst, b0[rows_]).then_inc(s["h_qkT"], 1)

    @block.sync
    def _(sp):
        def load(dst, src, sem):
            sp.dma_start(dst, src).then_inc(s[sem], 16)

        load(ids[:], dr["idsT"], "ids_in")
        load(wqT, rows(dr["L0_attn_wqT"], KD), "w0_in")
        load(wkT, rows(dr["L0_attn_wkT"], KD), "w0_in")
        load(w_vs, rows(dr["L0_attn_wvT"], KD), "w0_in")
        load(typ_i[:], dr["typesT"], "small_in")
        load(pos_t, dr["L0_tok_pos_emb"], "small_in")
        load(t01[:, 0, :], dr["L0_tok_type_emb"][0, :].partition_broadcast(P), "small_in")
        load(t01[:, 1, :], dr["L0_tok_type_emb"][1, :].partition_broadcast(P), "small_in")
        load(gam, dr["L0_tok_gamma"].partition_broadcast(P), "small_in")
        load(bet, dr["L0_tok_beta"].partition_broadcast(P), "small_in")
        load(ident[:], dr["ident"], "small_in")
        load(cst[:], dr["cst"], "small_in")
        load(w_q, rows(dr["L0_ffn_Wq"], KD), "wf_in")
        load(w_down, rows(dr["L0_ffn_Wdown"], KD), "wf_in")
        load(w_up, dr["L0_ffn_Wup"], "wf_in")
        load(w_o0, rows(dr["L0_ffn_Wo"], KD), "wf_in")
        load(w_g, rows(dr["L0_ffn_Wg"], KD), "wf_in")
        load(col[:, 0:2], dr["gamma1T"], "wf_in")
        load(col[:, 2:4], dr["gamma2T"], "wf_in")
        load(col[0:LAT, 4:5], dr["bdownT"], "wf_in")
        load(b_q, dr["L0_ffn_bq"].partition_broadcast(P), "wf_in")
        load(b_up, dr["L0_ffn_bup"].partition_broadcast(P), "wf_in")
        load(b_o, dr["L0_ffn_bo"].partition_broadcast(P), "wf_in")
        load(b_g, dr["L0_ffn_bg"].partition_broadcast(P), "wf_in")
        for e in range(E):
            load(w_e[:, :, e * D:(e + 1) * D], rows(dr["L0_ffn_We"][e], KD), "wf_in")
        load(w_qk1[:, :, 0:D], rows(dr["L1_attn_WqT"], KD), "w1_in")
        load(w_qk1[:, :, D:2 * D], rows(dr["L1_attn_WkT"], KD), "w1_in")
        load(w_v1, rows(dr["L1_attn_WvT"], KD), "w1_in")
        load(w_o1, rows(dr["L1_attn_WoT"], KD), "w1_in")
        load(w_router[:], rows(dr["routerT"], KD), "w1_in")
        load(cosb, dr["cos"], "w1_in")
        load(sinb, dr["sin"], "w1_in")

        def load_expert(e):
            gu = W[:, e, 0:GU].rearrange("p (k g i) -> p k g i", k=KD, g=2)
            load(gu[:, :, 0, :], rows(dr["gateT"][e], KD), "experts_in")
            load(gu[:, :, 1, :], rows(dr["upT"][e], KD), "experts_in")
            wd = W[:, e, GU:WE].rearrange("p (k d) -> p k d", k=KI)
            load(wd[:, 0:KI - 1, :], rows(dr["downT"][e, 0:(KI - 1) * P, :], KI - 1), "experts_in")
            load(wd[0:IR, KI - 1, :], dr["downT"][e, (KI - 1) * P:I, :], "experts_in")

        def maxima_into_q(t, u):
            sp.wait_ge(s["h_nTs"], t + 1)
            for f in range(2):
                for a in range(2):
                    r = NB * (2 * f + a)
                    sp.dma_start(qT[u][64 * f + PART + a:64 * f + PART + a + 1, :, :].bitcast(F32), nmT[r:r + NB, :].bitcast(F32)).then_inc(s["h_aug"], 16)

        sp.wait_ge(s["c_acc"], B)
        for e in range(5):
            load_expert(e)

        def step_d(i, pi):
            t = at(i, 5)
            if t is not None:
                maxima_into_q(t, (pi - 5) % 2)
            t = at(i, 9)
            if t is not None:
                u = (pi - 9) % 2
                sp.wait_ge(s["e_xn"], t + 1)
                lo = t * P
                sp.dma_start(xn_dram[bass.ds(lo, P), :], en[u]).then_inc(s[f"e_xout{u}"], 16)
                sp.dma_start(h_dram[bass.ds(lo, P), :], tile(h, t)).then_inc(s["e_hout"], 16)

        skewed(sp, step_d, B, 10)
        sp.wait_ge(s["e_lgs"], B)
        sp.wait_ge(s["h_upd"], B)
        sp.wait_ge(s["e_xout0"], 8 * B)
        sp.wait_ge(s["e_xout1"], 8 * B)
        for e in range(5, 8):
            load_expert(e)

    @block.gpsimd
    def _(pool):
        pool.wait_ge(s["ids_in"], 16)
        for t in range(B):
            pool.indirect_dma_start(h[:, t, :], None, dr["L0_tok_word_emb"],
                                    bass.IndirectOffsetOnAxis(ap=ids[:, t:t + 1], axis=0)
                                    ).then_inc(s["rows_in"], 16)
        pool.memset(neghalf[:], -0.5).then_inc(s["p_set"], 1)
        pool.memset(nms[:].bitcast(F32), 0.0).then_inc(s["p_set"], 1)
        for u in range(2):
            for f in range(2):
                pool.memset(kT[u][f][:].bitcast(F32), 0.0).then_inc(s["p_set"], 1)
        pool.memset(pad[:].bitcast(F32), 0.0).then_inc(s["p_set"], 1)
        for u in range(2):
            pool.memset(vaug[u], 0.0).then_inc(s["p_set"], 1)
        pool.memset(mask_qk[:], 0.0).then_inc(s["p_set"], 1)
        pool.memset(mask_kq[:], 0.0).then_inc(s["p_set"], 1)
        pool.memset(before[:], 1.0).then_inc(s["p_set"], 1)
        pool.memset(ones_b[:], 1.0).then_inc(s["p_set"], 1)
        pool.wait_ge(s["p_set"], 13)
        pool.memset(pad[:, 1, :, PART:AUG].bitcast(F32), 1.0).then_inc(s["masks"], 1)
        for u in range(2):
            pool.memset(vaug[u][:, :, HD:HD + 1], 1.0).then_inc(s["masks"], 1)
        pool.affine_select(out=mask_qk[:], in_=mask_qk[:], compare_op=ALU.is_ge, fill=NEG, base=0,
                           pattern=[[-1, P]], channel_multiplier=1).then_inc(s["masks"], 1)
        pool.affine_select(out=mask_kq[:], in_=mask_kq[:], compare_op=ALU.is_ge, fill=NEG, base=0,
                           pattern=[[1, P]], channel_multiplier=-1).then_inc(s["masks"], 1)
        pool.affine_select(out=before[:], in_=before[:], compare_op=ALU.is_gt, fill=0.0, base=0,
                           pattern=[[1, P]], channel_multiplier=-1).then_inc(s["masks"], 1)

        def rstd(x, u, t, eps):
            n, base = NORMS[x]
            count = ready(pool, base + t + 1)
            pool.wait_ge(s["masks"], 6)
            pool.wait_ge(s[f"n{n}_ag"], count)
            pool.tensor_scalar(rs[n][u][:, 0:1], mv[n][u][:, 1:2], eps, None, ALU.add).then_inc(s[f"n{n}_ep"], 1)
            power(n, base + t, u)

        def rrms(x, u, t, eps):
            n, base = NORMS[x]
            count = ready(pool, base + t + 1)
            pool.wait_ge(s["masks"], 6)
            pool.wait_ge(s[f"n{n}_ag"], count)
            pool.tensor_scalar(rs[n][u][:, 0:1], mv[n][u][:, 0:1], 1.0 / D, eps, ALU.mult, ALU.add
                               ).then_inc(s[f"n{n}_ep"], 1)
            power(n, base + t, u)

        def power(n, done, u):
            pool.wait_ge(s[f"n{n}_ep"], done + 1)
            pool.tensor_tensor(rs[n][u][:, 1:2], rs[n][u][:, 0:1], neghalf[:], ALU.pow).then_inc(s[f"n{n}_rs"], 1)

        def step_a(i, pi):
            t = at(i, 1)
            if t is not None:
                rstd("a1", (pi - 1) % 2, t, 1e-5)
            t = at(i, 0)
            if t is not None:
                rstd("a0", pi, t, 1e-12)

        def dup(t):
            count = ready(pool, t + 1)
            pool.wait_ge(s["masks"], 6)
            pool.wait_ge(s["h_hi"], count)
            pool.tensor_copy(pad[:, 0, :, 2 * HD:3 * HD], pad[:, 0, :, 0:HD]).then_inc(s["h_dup"], 1)
            pool.tensor_copy(pad[:, 1, :, HD:2 * HD], pad[:, 1, :, 0:HD]).then_inc(s["h_dup"], 1)

        def values(t, u):
            pool.wait_ge(s["d_vf"], t + 1)
            if due(t - 1):
                pool.wait_ge(s["h_AV"], t - 1)
            pool.tensor_copy(vaug[u][:, :, 0:HD], tile(v_tiles, t).rearrange("p (h d) -> p h d", h=H)
                             ).then_inc(s["h_va"], 1)

        def step_b(i, pi):
            t = at(i, 6)
            if t is not None:
                u = pi % 2
                pool.wait_ge(s["g_exp"], t + 1)
                if due(2 * t):
                    pool.wait_ge(s["g_O"], 2 * t)
                pool.tensor_tensor(heads3(pv)[:, 0:HP], over_keys(sc[u][:, 0:HP]), over_queries(tile(v_tiles, t), HP),
                                   ALU.mult).then_inc(s["g_pv_pool"], 1)
            t = at(i, 4)
            if t is not None:
                u = pi % 2
                pool.wait_ge(s["b_qf"], t + 1)
                pool.wait_ge(s["b_kf"], t + 1)
                for g in range(4):
                    if due(4 * (t - 1) + g + 1):
                        pool.wait_ge(s["g_S"], 4 * (t - 1) + g + 1)
                    pool.tensor_tensor(heads3(qk)[:, 4 * g:4 * g + 4],
                                       qkf[u][:, 0, 4 * g:4 * g + 4].unsqueeze(2).to_broadcast([P, 4, H, HD]),
                                       qkf[u][:, 1].unsqueeze(1).to_broadcast([P, 4, H, HD]), ALU.mult
                                       ).then_inc(s["g_qk_mul"], 1)
            t = at(i, 8)
            if t is not None:
                rrms("c0", pi % 2, t, 1e-6)
            t = at(i, 1)
            if t is not None:
                rrms("b1", (pi - 1) % 2, t, 1e-6)
            t = at(i, 0)
            if t is not None:
                rstd("b0", pi, t, 1e-5)

        def step_d(i, pi):
            t = at(i, 8)
            if t is not None:
                rstd("e1", pi % 2, t, 1e-5)
            t = at(i, 5)
            if t is not None:
                values(t, (pi - 5) % 2)
            t = at(i, 3)
            if t is not None:
                dup(t)
            t = at(i, 2)
            if t is not None:
                u = pi % 2
                pool.wait_ge(s["d_rot"], 3 * t + 3)
                if due(2 * (t - 1)):
                    pool.wait_ge(s["h_lo"], 2 * (t - 1))
                if due(t - 1):
                    pool.wait_ge(s["h_hi"], t - 1)
                pool.tensor_tensor(qkf[u].rearrange("p a h d -> p (a h d)"), t1.rearrange("p h d -> p (h d)"),
                                   t2.rearrange("p h d -> p (h d)"), ALU.add).then_inc(s["d_qf"], 1)
            t = at(i, 0)
            if t is not None:
                rstd("d0", pi, t, 1e-5)

        skewed(pool, step_a, B, 6)
        pool.wait_ge(s["a_done"], B)
        skewed(pool, step_b, B, 11)
        pool.wait_ge(s["c_acc"], B)
        skewed(pool, step_d, B, 10)

        def index(dst, row, j, name):
            pool.tensor_copy(dst, idx_i[:, row, bass.ds(j, 1)]).then_inc(s[name], 1)
            count = ready(pool, j + 1)
            pool.wait_ge(s["r_tables"], 1)
            pool.wait_ge(s[name], count)

        def step_f(i, pi):
            j = at(i, 4, NJ)
            if j is not None:
                u = pi % 2
                if due(8 * (j - u)):
                    pool.wait_ge(s[f"f_out{u}"], 8 * (j - u))
                index(si[u][:], 1, j, "f_si")
                count = ready(pool, j + 1)
                pool.wait_ge(s["r_tables"], 1)
                pool.wait_ge(s["f_y"], count)
                pool.indirect_dma_start(out, bass.IndirectOffsetOnAxis(ap=si[u][:], axis=0), yo[u], None,
                                        bounds_check=B * P - 1, oob_is_err=False).then_inc(s[f"f_out{u}"], 16)
            j = at(i, 3, NJ)
            if j is not None:
                u = (pi - 3) % 2
                if due(8 * (j - u)):
                    pool.wait_ge(s[f"f_hin{u}"], 8 * (j - u))
                index(hi_[u][:], 0, j, "f_hi")
                if due(j - 1):
                    count = ready(pool, j - 1)
                    pool.wait_ge(s["r_tables"], 1)
                    pool.wait_ge(s["f_y"], count)
                pool.indirect_dma_start(gh[u], None, h_dram, bass.IndirectOffsetOnAxis(ap=hi_[u][:], axis=0)
                                        ).then_inc(s[f"f_hin{u}"], 16)
            j = at(i, 0, NJ)
            if j is not None:
                u = pi
                if due(8 * (j - u)):
                    pool.wait_ge(s[f"f_xin{u}"], 8 * (j - u))
                index(gi[u][:], 0, j, "f_gi")
                if due(j - 1):
                    count = ready(pool, j - 1)
                    pool.wait_ge(s["r_tables"], 1)
                    pool.wait_ge(s["f_T"], count)
                pool.indirect_dma_start(gx[u], None, xn_dram, bass.IndirectOffsetOnAxis(ap=gi[u][:], axis=0)
                                        ).then_inc(s[f"f_xin{u}"], 16)

        pool.wait_ge(s["r_tables"], 1)
        pool.wait_ge(s["e_xout0"], 8 * B)
        pool.wait_ge(s["e_xout1"], 8 * B)
        pool.wait_ge(s["e_hout"], 16 * B)
        skewed(pool, step_f, NJ, 5)
        pool.wait_ge(s["f_out0"], 16 * ((NJ + 1) // 2))
        pool.wait_ge(s["f_out1"], 16 * (NJ // 2))

    @block.tensor
    def _(pe):
        def transpose(dst, src, k, sem, count=1):
            for n in range(k):
                ins = pe.transpose(dst[:, n * P:(n + 1) * P], src[:, n * P:(n + 1) * P], ident[:])
            ins.then_inc(s[sem], 1)

        def product(dst, lhsT, rhs, sem):
            for n, (a, b) in enumerate(zip(lhsT, rhs)):
                ins = pe.matmul(dst, a, b, start=n == 0, stop=n == len(lhsT) - 1)
            if sem:
                ins.then_inc(s[sem], 1)

        def kt(x, lo=0, hi=None):
            return [x[:, k, lo:hi if hi else x.shape[2]] for k in range(x.shape[1])]

        pe.wait_ge(s["w0_in"], 48)
        for c in range(KD):
            product(PS[:, c, 0:D], kt(wqT, c * P, (c + 1) * P), kt(wkT), "wa_ps")

        def step_a(i, pi):
            t = at(i, 5)
            if t is not None:
                u = (pi - 5) % 2
                pe.wait_ge(s["a_vn"], t + 1)
                pe.wait_ge(s["a_E"], t + 1)
                if due(t):
                    pe.wait_ge(s["a_done"], t)
                product(b4[:, 0:D], [ET[u]], [vn], "a_O")
            t = at(i, 4)
            if t is not None:
                u = pi % 2
                pe.wait_ge(s["a_uT"], t + 1)
                if due(t):
                    pe.wait_ge(s["a_E"], t)
                product(b1[:, 0:P], kt(xT[u]), kt(uT[u]), "a_S")
            t = at(i, 3)
            if t is not None:
                u = (pi - 3) % 2
                pe.wait_ge(s["a_xT"], t + 1)
                if due(t):
                    pe.wait_ge(s["a_uT"], t)
                for d in range(KD):
                    product(b3[:, d * P:(d + 1) * P], kt(w_a, d * P, (d + 1) * P), kt(xT[u]),
                            "a_u" if d == KD - 1 else None)
                if due(t):
                    pe.wait_ge(s["a_vs"], t)
                product(b7[:, 0:D], kt(xT[u]), kt(w_vs), "a_v")
            t = at(i, 2)
            if t is not None:
                pe.wait_ge(s["a_xn"], t + 1)
                if due(t):
                    pe.wait_ge(s["a_xT"], t)
                transpose(b6, xn[pi % 2], KD, "a_T")

        pe.wait_ge(s["small_in"], 16 * 8)
        pe.wait_ge(s["wa"], 2)
        pe.wait_ge(s["wv_s"], 2)
        skewed(pe, step_a, B, 6)

        def heads(i, pi):
            t4, t5, t6 = at(i, 4), at(i, 5), at(i, 6)
            u4, u5, u6 = pi % 2, (pi - 5) % 2, pi % 2

            def masked(bank, mask):
                pe.matmul(bank, ident_b[:], mask[:].unsqueeze(1).to_broadcast([P, 4, P]), start=True, stop=False,
                          skip_group_check=True)

            for g in range(6):
                if t6 is not None and g < 4:
                    if g == 0:
                        pe.wait_ge(s["h_aug"], 64 * (t6 + 1))
                        if due(done(i, 8)):
                            pe.wait_ge(s["h_upd"], done(i, 8))
                    if due(4 * t6 + g):
                        pe.wait_ge(s["h_exp"], 4 * t6 + g)
                    masked(b2, mask_kq)
                    for j in range(4):
                        blk, f = 4 * (g % 2) + j, g // 2
                        ins = pe.matmul(b2[:, j * P:(j + 1) * P], kT[u6][f][:, blk, :], qT[u6][:, blk, :],
                                        start=False, stop=True, skip_group_check=True)
                    ins.then_inc(s["h_S2"], 1)
                if t5 is not None and g < 4:
                    if g == 0:
                        pe.wait_ge(s["h_qkT"], 6 * (t5 + 1))
                        if due(done(i, 8)):
                            pe.wait_ge(s["h_oTs"], done(i, 8))
                        if due(done(i, 10)):
                            pe.wait_ge(s["e_xT"], done(i, 10))
                    if due(4 * t5 + g):
                        pe.wait_ge(s["h_max"], 4 * t5 + g)
                    masked(b1, mask_qk)
                    for j in range(4):
                        blk, f = 4 * (g % 2) + j, g // 2
                        ins = pe.matmul(b1[:, j * P:(j + 1) * P], qT[u5][:, blk, :], kT[u5][f][:, blk, :],
                                        start=False, stop=True, skip_group_check=True)
                    ins.then_inc(s["h_S1"], 1)
                if t4 is not None and g >= 2:
                    r = g - 2
                    if r == 0:
                        for name in ("dup", "lo"):
                            pe.wait_ge(s[f"h_{name}"], 2 * (t4 + 1))
                    if due(6 * t4 + (0, 1, 2, 4)[r]):
                        pe.wait_ge(s["h_qkT"], 6 * t4 + (0, 1, 2, 4)[r])
                    for n in range(4):
                        hd = 2 * (4 * (r % 2) + n)
                        ins = pe.transpose(b0[:, n * P:(n + 1) * P],
                                           pad[:, r // 2, hd:hd + 2, :].rearrange("p a b -> p (a b)").bitcast(F32),
                                           ident[:])
                    ins.then_inc(s["h_padT"], 1)
                if t6 is not None and 1 <= g < 5:
                    if g == 1:
                        pe.wait_ge(s["h_va"], t6 + 1)
                        if due(t6):
                            pe.wait_ge(s["h_o"], t6)
                    if due(4 * t6 + g):
                        pe.wait_ge(s["h_exp"], 4 * t6 + g)
                    for j in range(4):
                        slot = 4 * (g - 1) + j
                        hd = slot % NB * 2 + slot // NB
                        ins = pe.matmul(b4[32 * j:32 * (j + 1), (g - 1) * P:g * P], vaug[u6][:, hd, :], PT[:, slot, :],
                                        start=True, stop=True)
                    if g == 4:
                        ins.then_inc(s["h_AV"], 1)

        def heads_out_T(t):
            pe.wait_ge(s["h_OTs"], t + 1)
            transpose(b4, ots, 4, "h_OTT")

        def normed_T(i, t):
            pe.wait_ge(s["h_o"], t + 1)
            if due(4 * done(i, 5)):
                pe.wait_ge(s["h_max"], 4 * done(i, 5))
            transpose(b1, o_sb, KD, "h_oT")

        def project_out(i, t, w):
            pe.wait_ge(s["h_oTs"], t + 1)
            if due(4 * done(i, 6)):
                pe.wait_ge(s["h_exp"], 4 * done(i, 6))
            product(b2[:, 0:D], kt(oT), kt(w), "h_Wo")

        def maxima_T(i, t):
            pe.wait_ge(s["h_nl"], t + 1)
            if due(t):
                pe.wait_ge(s["h_nTs"], t)
            if due(done(i, 10)):
                pe.wait_ge(s["e_lgs"], done(i, 10))
            pe.transpose(b5[:, P:2 * P], nms[:].bitcast(F32), ident[:]).then_inc(s["h_nT"], 1)

        def step_b(i, pi):
            t2, t3, t8, t9, t10 = (at(i, k) for k in (2, 3, 8, 9, 10))

            def experts(r):
                if due(E * t10 + 2 * r - 2):
                    pe.wait_ge(s["c_es"], E * t10 + 2 * r - 2)
                if r < 2:
                    if due(E * t10):
                        pe.wait_ge(s["c_es"], E * t10)
                product(PS[:, r % 2, :], kt(eT[pi % 2]), kt(w_e, 2 * r * D, 2 * (r + 1) * D), "c_exp")

            def summed(r):
                if r == 0:
                    if due(t10):
                        pe.wait_ge(s["c_acc"], t10)
                    pe.matmul(b2[:, 0:D], ident[:], tile(x2, t10), start=True, stop=False)
                    pe.matmul(b2[:, 0:D], ident[:], tile(h, t10), start=False, stop=False)
                for e in (2 * r, 2 * r + 1):
                    pe.wait_ge(s["c_es"], E * t10 + e + 1)
                    ins = pe.matmul(b2[:, 0:D], ident[:], es[:, e, :], start=False, stop=e == E - 1)
                ins.then_inc(s["c_sum"], 1)

            if t8 is not None:
                pe.wait_ge(s["g_o"], t8 + 1)
                if due(t8):
                    pe.wait_ge(s["g_upd"], t8)
                transpose(b4[:, D:2 * D], o_sb, KD, "g_oT")
            if t3 is not None:
                u = (pi - 3) % 2
                pe.wait_ge(s["b_xT"], t3 + 1)
                if due(t3):
                    pe.wait_ge(s["b_qf"], t3)
                pe.matmul(b7[:, 0:D], ident[:], b_q, start=True, stop=False)
                for k in range(KD):
                    ins = pe.matmul(b7[:, 0:D], xT[u][:, k, :], w_q[:, k, :], start=False, stop=k == KD - 1)
                ins.then_inc(s["b_q"], 1)
                if due(done(i, 10)):
                    pe.wait_ge(s["c_lb"], done(i, 10))
                product(b5[0:LAT, 0:P], kt(w_down), kt(xT[u]), "b_c")
            if t10 is not None:
                pe.wait_ge(s["c_xT"], t10 + 1)
                experts(0)
                experts(1)
            if t8 is not None:
                pe.wait_ge(s["g_oTs"], t8 + 1)
                pe.matmul(b4[:, 0:D], ident[:], tile(x2, t8), start=True, stop=False)
                pe.matmul(b4[:, 0:D], ident[:], b_o, start=False, stop=False)
                for k in range(KD):
                    ins = pe.matmul(b4[:, 0:D], oT[:, k, :], w_o0[:, k, :], start=False, stop=k == KD - 1)
                ins.then_inc(s["g_Wo"], 1)
            if t3 is not None:
                pe.wait_ge(s["b_cT"], t3 + 1)
                if due(t3):
                    pe.wait_ge(s["b_vf"], t3)
                product(b3, [cT], [w_up], "b_kv")
            if t10 is not None:
                summed(0)
                experts(2)
                summed(1)
                experts(3)
            if t9 is not None:
                pe.wait_ge(s["c_xn"], t9 + 1)
                transpose(b6[:, D:2 * D], en[(pi - 9) % 2], KD, "c_T")
            if t10 is not None:
                summed(2)
            if t9 is not None:
                pe.wait_ge(s["c_xT"], t9 + 1)
                if due(done(i, 3)):
                    pe.wait_ge(s["b_cT"], done(i, 3))
                product(b5[:, P:P + E], kt(eT[(pi - 9) % 2]), kt(w_g), "c_lg")
            if t2 is not None:
                pe.wait_ge(s["b_xn"], t2 + 1)
                transpose(b6, xn[pi % 2], KD, "b_T")
            if t10 is not None:
                summed(3)

        pe.wait_ge(s["a_done"], B)
        pe.wait_ge(s["wf_s"], 4)
        skewed(pe, step_b, B, 11)

        def step_d(i, pi):
            t2, t5, t7 = at(i, 2), at(i, 5), at(i, 7)
            if t7 is not None:
                heads_out_T(t7)
            heads(i, pi)
            if t5 is not None:
                maxima_T(i, t5)
            if t7 is not None:
                normed_T(i, t7)
            if t2 is not None:
                u = pi % 2
                pe.wait_ge(s["d_xT"], t2 + 1)
                if due(3 * t2):
                    pe.wait_ge(s["d_rot"], 3 * t2)
                product(b3, kt(xT[u]), kt(w_qk1), "d_qk")
                if due(t2):
                    pe.wait_ge(s["d_vf"], t2)
                product(b7[:, 0:D], kt(xT[u]), kt(w_v1), "d_v")
            if t7 is not None:
                project_out(i, t7, w_o1)
            t = at(i, 1)
            if t is not None:
                pe.wait_ge(s["d_xn"], t + 1)
                if due(t):
                    pe.wait_ge(s["d_xT"], t)
                transpose(b6, xn[(pi - 1) % 2], KD, "d_T")
            t = at(i, 9)
            if t is not None:
                pe.wait_ge(s["e_xn"], t + 1)
                if due(done(i, 7)):
                    pe.wait_ge(s["h_oTs"], done(i, 7))
                if due(4 * done(i, 5)):
                    pe.wait_ge(s["h_max"], 4 * done(i, 5))
                transpose(b1[:, D:2 * D], en[(pi - 9) % 2], KD, "e_T")
                pe.wait_ge(s["e_xT"], t + 1)
                if due(done(i, 5)):
                    pe.wait_ge(s["h_nTs"], done(i, 5))
                product(b5[:, 0:E], kt(eT[0]), kt(w_router), "e_lg")

        pe.wait_ge(s["c_acc"], B)
        pe.wait_ge(s["masks"], 6)
        pe.wait_ge(s["ident_b"], 1)
        pe.wait_ge(s["w1_in"], 16 * 7)
        skewed(pe, step_d, B, 10)

        pe.wait_ge(s["e_lgs"], B)
        pe.wait_ge(s["r_dve"], 6)
        hot = r_hot_b
        pe.matmul(b0[:, 0:B * E], before[:], hot.rearrange("p b e -> p (b e)"), start=True, stop=False,
                  skip_group_check=True)
        for d in range(1, B):
            pe.matmul(b0[:, d * E:B * E], ones_b[:], hot[:, 0:B - d, :].rearrange("p b e -> p (b e)"),
                      start=False, stop=d == B - 1, skip_group_check=True)
        for t in range(B):
            ins = pe.matmul(b1[:, 0:E], ones_b[:], hot[:, t, :], start=t == 0, stop=t == B - 1)
        ins.then_inc(s["r_pe"], 1)
        pe.wait_ge(s["r_hots"], 1)
        for t in range(B):
            ins = pe.matmul(b2[:, 0:NJ], r_hot_c[:, t, :], r_hot_a[:, t, :], start=t == 0, stop=t == B - 1)
        ins.then_inc(s["r_pe"], 1)

        def step_f(i, pi):
            j4, j3, j2, j1 = (at(i, k, NJ) for k in (4, 3, 2, 1))
            if j4 is not None:
                u = pi % 2
                e = pe.value_load(texp_i[0:1, bass.ds(j4, 1)], min_val=0, max_val=E - 1)
                pe.wait_ge(s["f_hTa"], j4 + 1)
                pe.wait_ge(s["f_hTb"], j4 + 1)
                if due(j4):
                    pe.wait_ge(s["f_y"], j4)
                for k in range(KI):
                    r = P if k < KI - 1 else IR
                    w = W[0:r, bass.ds(e, 1), GU + k * D:GU + (k + 1) * D].rearrange("p a d -> p (a d)")
                    ins = pe.matmul(b7[:, 0:D], hT[u][0:r, k, :], w, start=k == 0, stop=k == KI - 1)
                ins.then_inc(s["f_down"], 1)
            if j2 is not None:
                u = pi % 2
                e = pe.value_load(texp_i[0:1, bass.ds(j2, 1)], min_val=0, max_val=E - 1)
                pe.wait_ge(s["f_xT"], j2 + 1)
                for half, (name, free_name) in enumerate((("f_gate", "f_silu"), ("f_up", "f_hm"))):
                    if due(j2):
                        pe.wait_ge(s[free_name], j2)
                    for n in range(2):
                        for k in range(KD):
                            lo = (k * 2 + half) * I + n * IH
                            w = W[:, bass.ds(e, 1), lo:lo + IH].rearrange("p a d -> p (a d)")
                            ins = pe.matmul(PS[:, 1 + 2 * half + n, 0:IH], xsT[u][:, k, :], w,
                                            start=k == 0, stop=k == KD - 1)
                    ins.then_inc(s[name], 1)
            if j3 is not None:
                u = (pi - 3) % 2
                pe.wait_ge(s["f_hm"], j3 + 1)
                for bank, name, done in ((b5, "f_Ta", "f_hTa"), (b6, "f_Tb", "f_hTb")):
                    if due(j3):
                        pe.wait_ge(s[done], j3)
                    for n in range(3):
                        k = n if bank is b5 else n + 3
                        w = P if k < KI - 1 else IR
                        ins = pe.transpose(bank[0:w, n * P:(n + 1) * P], hm[u][:, k * P:k * P + w], ident[:])
                    ins.then_inc(s[name], 1)
            if j1 is not None:
                u = (pi - 1) % 2
                pe.wait_ge(s[f"f_xin{u}"], 8 * (j1 - u) + 16)
                if due(j1):
                    pe.wait_ge(s["f_xT"], j1)
                transpose(b0, gx[u], KD, "f_T")

        pe.wait_ge(s["experts_in"], 16 * 4 * E)
        pe.wait_ge(s["r_tables"], 1)
        skewed(pe, step_f, NJ, 5)

    @block.scalar
    def _(act):
        def copy(dst, src, sem, **k):
            act.activation(dst, src, ACT.Copy, **k).then_inc(s[sem], 1)

        for k in range(KD):
            act.wait_ge(s["wv_mx"], k + 1)
            act.activation(w_vs[:, k, :], w_vs[:, k, :], ACT.Exp, bias=wv_small[:, k:k + 1],
                           accum_out=wv_small[:, 2 + k:3 + k]).then_inc(s["wv_ex"], 1)
        for c in range(KD):
            act.wait_ge(s["wa_ps"], c + 1)
            copy(w_a[:, c, :], PS[:, c, 0:D], "wa")

        def step_a(i, pi):
            t = at(i, 4)
            if t is not None:
                u = pi % 2
                act.wait_ge(s["a_mx"], t + 1)
                if due(t - 1):
                    act.wait_ge(s["a_O"], t - 1)
                act.activation(ET[u], b1[:, 0:P], ACT.Exp, bias=sm[u][:, 0:1], scale=SCALE0,
                               accum_out=sm[u][:, 1:2]).then_inc(s["a_E"], 1)
            t = at(i, 3)
            if t is not None:
                act.wait_ge(s["a_v"], t + 1)
                if due(t - 1):
                    act.wait_ge(s["a_hv"], t - 1)
                copy(va_[(pi - 3) % 2], b7[:, 0:D], "a_vs")
            t = at(i, 2)
            if t is not None:
                act.wait_ge(s["a_T"], t + 1)
                if due(t - 1):
                    act.wait_ge(s["a_S"], t - 1)
                copy(xT[pi % 2].rearrange("p k t -> p (k t)"), b6[:, 0:D], "a_xT")

        skewed(act, step_a, B, 6)

        def heads(i, pi):
            t4, t6 = at(i, 4), at(i, 6)
            for g in range(6):
                if t6 is not None and g < 4:
                    act.wait_ge(s["h_S2"], 4 * t6 + g + 1)
                    if due(t6):
                        act.wait_ge(s["h_AV"], t6)
                    act.activation(PT[:, 4 * g:4 * g + 4, :].rearrange("p h t -> p (h t)"), b2, ACT.Exp,
                                   scale=SCALEH).then_inc(s["h_exp"], 1)
                if t4 is not None and g == 2:
                    qk_out(act, t4, pi % 2, 0)
                if t4 is not None and g >= 4:
                    qk_out(act, t4, pi % 2, g - 2, 0)
            if t6 is not None:
                act.wait_ge(s["h_AV"], t6 + 1)
                if due(t6):
                    act.wait_ge(s["h_OTT"], t6)
                copy(ots, b4, "h_OTs")

        def after(i, pi):
            t = at(i, 7)
            if t is not None:
                act.wait_ge(s["h_oT"], t + 1)
                if due(t):
                    act.wait_ge(s["h_Wo"], t)
                copy(oT.rearrange("p k t -> p (k t)"), b1[:, 0:D], "h_oTs")

        def maxima(i):
            t = at(i, 5)
            if t is not None:
                act.wait_ge(s["h_nT"], t + 1)
                if due(64 * t):
                    act.wait_ge(s["h_aug"], 64 * t)
                copy(nmT[:], b5[0:32, P:2 * P], "h_nTs")

        def high(t, u, name):
            act.wait_ge(s[name], t + 1)
            if due(4 * t):
                act.wait_ge(s["h_padT"], 4 * t)
            copy(pad[:, :, :, 0:HD], qkf[u], "h_hi")

        def step_b(i, pi):
            t1_, t2, t3, t5, t8, t9, t10 = (at(i, k) for k in (1, 2, 3, 5, 8, 9, 10))

            def by_gates(r):
                u = pi % 2
                if r == 0:
                    act.wait_ge(s["c_gt"], t10 + 1)
                act.wait_ge(s["c_exp"], 4 * t10 + r + 1)
                if due(4 * t10):
                    act.wait_ge(s["c_sum"], 4 * t10)
                for e in (2 * r, 2 * r + 1):
                    lo = e % 2 * D
                    copy(es[:, e, :], PS[:, r % 2, lo:lo + D], "c_es", scale=gate[u][:, e:e + 1])

            def squares(x, src, t, made):
                n, base = NORMS[x]
                free, before_, count = ready(act, base + t - 1), ready(act, base + t), ready(act, t + 1)
                act.wait_ge(s["wf_s"], 4)
                act.wait_ge(s[made], count)
                if due(free):
                    act.wait_ge(s[f"n{n}_rs"], free)
                if due(before_):
                    act.wait_ge(s[f"n{n}_ag"], before_)
                act.activation(ots[:, (n - 1) * D:n * D], src, ACT.Square, accum_out=mv[n][(pi - (n == 1)) % 2][:, 0:1]
                               ).then_inc(s[f"n{n}_ag"], 1)

            if t8 is not None:
                act.wait_ge(s["g_oT"], t8 + 1)
                if due(t8):
                    act.wait_ge(s["g_Wo"], t8)
                copy(oT.rearrange("p k t -> p (k t)"), b4[:, D:2 * D], "g_oTs")
            if t3 is not None:
                act.wait_ge(s["b_q"], t3 + 1)
                if due(4 * (t3 - 1)):
                    act.wait_ge(s["g_qk_mul"], 4 * (t3 - 1))
                copy(qkf[(pi - 3) % 2][:, 0].rearrange("p h d -> p (h d)"), b7[:, 0:D], "b_qf")
                act.wait_ge(s["b_c"], t3 + 1)
                if due(t3):
                    act.wait_ge(s["b_kv"], t3)
                act.activation(cT, b5[0:LAT, 0:P], ACT.Identity, bias=col[0:LAT, 4:5]).then_inc(s["b_cT"], 1)
            if t10 is not None:
                by_gates(0)
                by_gates(1)
            if t8 is not None:
                count = ready(act, t8 + 1)
                act.wait_ge(s["wf_s"], 4)
                act.wait_ge(s["g_Wo"], count)
                copy(tile(x2, t8), b4[:, 0:D], "g_upd")
                squares("c0", tile(x2, t8), t8, "g_upd")
            if t10 is not None:
                by_gates(2)
                by_gates(3)
            if t9 is not None:
                act.wait_ge(s["c_T"], t9 + 1)
                if due(4 * (t9 - 1)):
                    act.wait_ge(s["c_exp"], 4 * (t9 - 1))
                copy(eT[(pi - 9) % 2].rearrange("p k t -> p (k t)"), b6[:, D:2 * D], "c_xT")
            if t5 is not None:
                u = (pi - 5) % 2
                act.wait_ge(s["g_sub"], t5 + 1)
                act.activation(sc[u], sc[u], ACT.Exp, scale=SCALEH).then_inc(s["g_exp"], 1)
            if t2 is not None:
                act.wait_ge(s["b_T"], t2 + 1)
                if due(t2 - 1):
                    act.wait_ge(s["b_q"], t2 - 1)
                    act.wait_ge(s["b_c"], t2 - 1)
                copy(xT[pi % 2].rearrange("p k t -> p (k t)"), b6[:, 0:D], "b_xT")
            if t10 is not None:
                count = ready(act, 4 * t10 + 4)
                act.wait_ge(s["wf_s"], 4)
                act.wait_ge(s["c_sum"], count)
                copy(tile(h, t10), b2[:, 0:D], "c_acc")
            if t9 is not None:
                u = (pi - 9) % 2
                act.wait_ge(s["c_mx"], t9 + 1)
                if due(t9 - 1):
                    act.wait_ge(s["c_gt"], t9 - 1)
                act.activation(gate[u], glog, ACT.Exp, bias=gmax[:, 0:1], accum_out=gsum[u][:, 0:1]
                               ).then_inc(s["c_ex"], 1)
            if t1_ is not None:
                squares("b1", tile(x2, t1_), t1_, "b_x2")

        act.wait_ge(s["a_done"], B)
        act.wait_ge(s["wf_s"], 4)
        skewed(act, step_b, B, 11)

        def step_d(i, pi):
            heads(i, pi)
            maxima(i)
            after(i, pi)
            t = at(i, 3)
            if t is not None:
                high(t, (pi - 3) % 2, "d_qf")
            t = at(i, 2)
            if t is not None:
                act.wait_ge(s["d_v"], t + 1)
                copy(tile(v_tiles, t), b7[:, 0:D], "d_vf")
            t = at(i, 1)
            if t is not None:
                act.wait_ge(s["d_T"], t + 1)
                if due(t - 1):
                    act.wait_ge(s["d_v"], t - 1)
                copy(xT[(pi - 1) % 2].rearrange("p k t -> p (k t)"), b6[:, 0:D], "d_xT")
            t = at(i, 9)
            if t is not None:
                act.wait_ge(s["e_T"], t + 1)
                copy(eT[0].rearrange("p k t -> p (k t)"), b1[:, D:2 * D], "e_xT")
                act.wait_ge(s["e_lg"], t + 1)
                copy(tile(LG, t), b5[:, 0:E], "e_lgs")

        act.wait_ge(s["c_acc"], B)
        act.wait_ge(s["masks"], 6)
        skewed(act, step_d, B, 10)

        def step_f(i, pi):
            j = at(i, 2, NJ)
            if j is not None:
                act.wait_ge(s["f_gate"], j + 1)
                if due(j):
                    act.wait_ge(s["f_hm"], j)
                act.activation(sg.rearrange("p (n i) -> p n i", n=2), PS[:, 1:3, 0:IH], ACT.Silu
                               ).then_inc(s["f_silu"], 1)
            j = at(i, 3, NJ)
            if j is not None:
                act.wait_ge(s["f_Ta"], j + 1)
                if due(j - 1):
                    act.wait_ge(s["f_down"], j - 1)
                copy(hT[(pi - 3) % 2][:, 0:3, :].rearrange("p k t -> p (k t)"), b5[:, 0:3 * P], "f_hTa")

        act.wait_ge(s["r_tables"], 1)
        skewed(act, step_f, NJ, 5)

    @block.vector
    def _(dve):
        def stats(x, src, u, t):
            n = NORMS[x][0]
            dve.bn_stats(stat[n][:], src).then_inc(s[f"n{n}_st"], 1)
            count = ready(dve, TAKEN[x] + t + 1)
            dve.wait_ge(s["small_in"], 16 * 8)
            dve.wait_ge(s[f"n{n}_st"], count)
            dve.bn_aggr(mv[n][u][:], stat[n][:]).then_inc(s[f"n{n}_ag"], 1)

        def rs_ready(x, t):
            n, base = NORMS[x]
            dve.wait_ge(s[f"n{n}_rs"], base + t + 1)

        def normed(dst, src, n, u, sem):
            dve.tensor_scalar(dst, src, mv[n][u][:, 0:1], rs[n][u][:, 1:2], ALU.subtract, ALU.mult
                              ).then_inc(s[sem], 1)

        dve.wait_ge(s["w0_in"], 48)
        for k in range(KD):
            dve.tensor_reduce(wv_small[:, k:k + 1], w_vs[:, k, :], AX.X, ALU.max, negate=True).then_inc(s["wv_mx"], 1)
        for k in range(KD):
            dve.wait_ge(s["wv_ex"], k + 1)
            dve.reciprocal(wv_small[:, 4 + k:5 + k], wv_small[:, 2 + k:3 + k]).then_inc(s["wv_ri"], 1)
            dve.wait_ge(s["wv_ri"], k + 1)
            dve.tensor_scalar(w_vs[:, k, :], w_vs[:, k, :], wv_small[:, 4 + k:5 + k], 1.0 / D, ALU.mult, ALU.mult
                              ).then_inc(s["wv_s"], 1)
        dve.wait_ge(s["small_in"], 16 * 8)
        dve.tensor_copy(ident_b[:], ident[:]).then_inc(s["ident_b"], 1)
        dve.tensor_copy(typ, typ_i[:]).then_inc(s["prep"], 1)
        dve.tensor_tensor(pos_t, pos_t, t01[:, 0, :], ALU.add).then_inc(s["prep"], 1)
        dve.tensor_tensor(dtype_, t01[:, 1, :], t01[:, 0, :], ALU.subtract).then_inc(s["prep"], 1)
        dve.wait_ge(s["prep"], 3)
        dve.wait_ge(s["rows_in"], 16 * B)

        def step_a(i, pi):
            t = at(i, 5)
            if t is not None:
                u = (pi - 5) % 2
                dve.tensor_tensor(tile(h, t), tile(h, t), va_[u], ALU.subtract).then_inc(s["a_hv"], 1)
                dve.wait_ge(s["a_hv"], t + 1)
                dve.wait_ge(s["a_O"], t + 1)
                dve.tensor_tensor(tile(h, t), b4[:, 0:D], tile(h, t), ALU.add).then_inc(s["a_done"], 1)
            t = at(i, 4)
            if t is not None:
                u = pi % 2
                dve.wait_ge(s["a_S"], t + 1)
                dve.tensor_reduce(sm[u][:, 3:4], b1[:, 0:P], AX.X, ALU.max, negate=True).then_inc(s["a_mr"], 1)
                dve.wait_ge(s["a_mr"], t + 1)
                dve.tensor_scalar(sm[u][:, 0:1], sm[u][:, 3:4], SCALE0, None, ALU.mult).then_inc(s["a_mx"], 1)
            t = at(i, 3)
            if t is not None:
                dve.wait_ge(s["a_u"], t + 1)
                if due(t - 1):
                    dve.wait_ge(s["a_S"], t - 1)
                dve.tensor_copy(uT[(pi - 3) % 2].rearrange("p k t -> p (k t)"), b3[:, 0:D]).then_inc(s["a_uT"], 1)
            t = at(i, 2)
            if t is not None:
                rs_ready("a1", t)
                if due(t - 1):
                    dve.wait_ge(s["a_T"], t - 1)
                normed(xn[pi % 2], tile(h, t), 1, pi % 2, "a_xn")
            t = at(i, 4)
            if t is not None:
                u = pi % 2
                dve.wait_ge(s["a_E"], t + 1)
                dve.reciprocal(sm[u][:, 2:3], sm[u][:, 1:2]).then_inc(s["a_ri"], 1)
                dve.wait_ge(s["a_ri"], t + 1)
                dve.wait_ge(s["a_vs"], t + 1)
                if due(t):
                    dve.wait_ge(s["a_O"], t)
                dve.tensor_scalar(vn, va_[u], sm[u][:, 2:3], None, ALU.mult).then_inc(s["a_vn"], 1)
            t = at(i, 1)
            if t is not None:
                u = (pi - 1) % 2
                rs_ready("a0", t)
                normed(n0, tile(h, t), 0, u, "a_ng")
                dve.wait_ge(s["a_ng"], 2 * t + 1)
                dve.tensor_tensor(n0, n0, gam, ALU.mult).then_inc(s["a_ng"], 1)
                dve.wait_ge(s["a_ng"], 2 * t + 2)
                dve.tensor_tensor(tile(h, t), n0, bet, ALU.add).then_inc(s["a_h"], 1)
                count = ready(dve, t + 1)
                dve.wait_ge(s["small_in"], 16 * 8)
                dve.wait_ge(s["a_h"], count)
                stats("a1", tile(h, t), u, t)
            t = at(i, 0)
            if t is not None:
                dve.tensor_tensor(tile(h, t), tile(h, t), pos_t, ALU.add).then_inc(s["a_x"], 1)
                dve.wait_ge(s["a_x"], t + 1)
                dve.scalar_tensor_tensor(tile(h, t), dtype_, typ[:, bass.ds(t, 1)], tile(h, t), ALU.mult, ALU.add
                                         ).then_inc(s["a_xt"], 1)
                count = ready(dve, t + 1)
                dve.wait_ge(s["small_in"], 16 * 8)
                dve.wait_ge(s["a_xt"], count)
                stats("a0", tile(h, t), pi, t)

        skewed(dve, step_a, B, 6)
        dve.wait_ge(s["a_done"], B)

        def normalise(i):
            t = at(i, 7)
            if t is not None:
                dve.wait_ge(s["h_OTT"], t + 1)
                heads_ = b4.rearrange("p (h c) -> p h c", h=H)
                dve.reciprocal(rinv[:].unsqueeze(2), heads_[:, :, HD:HD + 1]).then_inc(s["h_ri"], 1)
                dve.wait_ge(s["h_ri"], t + 1)
                if due(t):
                    dve.wait_ge(s["h_oT"], t)
                dve.tensor_tensor(o_sb.rearrange("p (b f d) -> p f b d", f=2, d=HD),
                                  heads_[:, :, 0:HD].rearrange("p (f b) d -> p f b d", f=2),
                                  rinv[:].rearrange("p (f b) -> p f b", f=2).unsqueeze(3).to_broadcast([P, 2, NB, HD]),
                                  ALU.mult).then_inc(s["h_o"], 1)

        def heads(i, pi):
            t4, t5 = at(i, 4), at(i, 5)
            for g in range(6):
                if t5 is not None and g < 4:
                    dve.wait_ge(s["h_S1"], 4 * t5 + g + 1)
                    dve.tensor_reduce(nmax[:, 4 * g:4 * g + 4], b1.rearrange("p (h k) -> p h k", h=4), AX.X, ALU.max,
                                      negate=True).then_inc(s["h_max"], 1)
                if t5 is not None and g == 4:
                    split = nms[:, 0:32].rearrange("p (f a b) -> p f a b", f=2, a=2)
                    whole = nmax[:].rearrange("p (f b) -> p f b", f=2)
                    dve.wait_ge(s["h_max"], 4 * t5 + 4)
                    if due(t5):
                        dve.wait_ge(s["h_nT"], t5)
                    dve.tensor_copy(split[:, :, 0, :], whole).then_inc(s["h_nh"], 1)
                    dve.wait_ge(s["h_nh"], t5 + 1)
                    dve.tensor_tensor(split[:, :, 1, :], whole, split[:, :, 0, :].bitcast(F32), ALU.subtract
                                      ).then_inc(s["h_nl"], 1)
                if t4 is not None and g == 3:
                    qk_out(dve, t4, pi % 2, 1)
                if t4 is not None and g >= 4:
                    qk_out(dve, t4, pi % 2, g - 2, 1)

        def low(t, u):
            dve.wait_ge(s["h_hi"], t + 1)
            for x, at_ in ((0, HD), (1, 2 * HD)):
                dve.tensor_tensor(pad[:, x, :, at_:at_ + HD], qkf[u][:, x], pad[:, x, :, 0:HD].bitcast(F32),
                                  ALU.subtract).then_inc(s["h_lo"], 1)

        def step_b(i, pi):
            t1_, t2, t3, t5, t6, t7, t8, t9, t10 = (at(i, k) for k in (1, 2, 3, 5, 6, 7, 8, 9, 10))
            t0 = at(i, 0)
            if t10 is not None:
                u = pi % 2
                dve.wait_ge(s["c_ex"], t10 + 1)
                dve.reciprocal(gsum[u][:, 1:2], gsum[u][:, 0:1]).then_inc(s["c_ri"], 1)
                dve.wait_ge(s["c_ri"], t10 + 1)
                dve.tensor_scalar(gate[u], gate[u], gsum[u][:, 1:2], None, ALU.mult).then_inc(s["c_gt"], 1)
            if t7 is not None:
                u = (pi - 7) % 2
                for lo, hi, name in ((0, HP, "g_pv_pool"), (HP, H, "g_pv_dve")):
                    dve.wait_ge(s[name], t7 + 1)
                    if lo == 0:
                        if due(t7):
                            dve.wait_ge(s["g_oT"], t7)
                    dve.tensor_reduce(o_heads[:, lo:hi], heads3(pv)[:, lo:hi], AX.X, ALU.add).then_inc(s["g_O"], 1)
                dve.wait_ge(s["g_ri"], t7 + 1)
                dve.wait_ge(s["g_O"], 2 * t7 + 2)
                dve.tensor_tensor(o_heads, o_heads, rsum[u].unsqueeze(2).to_broadcast([P, H, HD]), ALU.mult
                                  ).then_inc(s["g_o"], 1)
            if t9 is not None:
                rs_ready("c0", t9)
                if due(t9 - 1):
                    dve.wait_ge(s["c_T"], t9 - 1)
                dve.tensor_scalar(en[(pi - 9) % 2], tile(x2, t9), rs[2][(pi - 9) % 2][:, 1:2], None, ALU.mult
                                  ).then_inc(s["c_xn"], 1)
            if t2 is not None:
                rs_ready("b1", t2)
                if due(t2 - 1):
                    dve.wait_ge(s["b_T"], t2 - 1)
                dve.tensor_scalar(xn[pi % 2], tile(x2, t2), rs[1][pi % 2][:, 1:2], None, ALU.mult
                                  ).then_inc(s["b_xn"], 1)
            if t1_ is not None:
                rs_ready("b0", t1_)
                normed(tile(x2, t1_), tile(h, t1_), 0, (pi - 1) % 2, "b_x2")
            if t5 is not None:
                u = (pi - 5) % 2
                for g in range(4):
                    dve.wait_ge(s["g_qk_mul"], 4 * t5 + g + 1)
                    if g == 0:
                        if due(t5 - 1):
                            dve.wait_ge(s["g_pv_pool"], t5 - 1)
                        if due(t5 - 1):
                            dve.wait_ge(s["g_pv_dve"], t5 - 1)
                        if due(t5 - 1):
                            dve.wait_ge(s["g_sum"], t5 - 1)
                    dve.tensor_reduce(sc[u][:, 4 * g:4 * g + 4], heads3(qk)[:, 4 * g:4 * g + 4], AX.X, ALU.add
                                      ).then_inc(s["g_S"], 1)
            if t5 is not None:
                dve.wait_ge(s["g_S"], 4 * t5 + 4)
                dve.tensor_reduce(hmax, sc[u], AX.X, ALU.max).then_inc(s["g_max"], 1)
                dve.wait_ge(s["g_max"], t5 + 1)
                dve.tensor_tensor(sc[u], sc[u], hmax.unsqueeze(2).to_broadcast([P, H, H]), ALU.subtract
                                  ).then_inc(s["g_sub"], 1)
            if t6 is not None:
                u = pi % 2
                dve.wait_ge(s["g_exp"], t6 + 1)
                if due(t6 - 1):
                    dve.wait_ge(s["g_o"], t6 - 1)
                dve.tensor_reduce(rsum[u], sc[u], AX.X, ALU.add).then_inc(s["g_sum"], 1)
                dve.wait_ge(s["g_sum"], t6 + 1)
                dve.reciprocal(rsum[u], rsum[u]).then_inc(s["g_ri"], 1)
                if due(2 * t6):
                    dve.wait_ge(s["g_O"], 2 * t6)
                dve.tensor_tensor(heads3(pv)[:, HP:H], over_keys(sc[u][:, HP:H]),
                                  over_queries(tile(v_tiles, t6), H - HP), ALU.mult).then_inc(s["g_pv_dve"], 1)
            if t3 is not None:
                u = (pi - 3) % 2
                kv = b3.rearrange("p (h c) -> p h c", h=H)
                bias = b_up.rearrange("p (h c) -> p h c", h=H)
                dve.wait_ge(s["b_kv"], t3 + 1)
                if due(4 * (t3 - 1)):
                    dve.wait_ge(s["g_qk_mul"], 4 * (t3 - 1))
                dve.tensor_tensor(qkf[u][:, 1], kv[:, :, 0:HD], bias[:, :, 0:HD], ALU.add).then_inc(s["b_kf"], 1)
                dve.tensor_tensor(over_heads(tile(v_tiles, t3)), kv[:, :, HD:2 * HD], bias[:, :, HD:2 * HD], ALU.add
                                  ).then_inc(s["b_vf"], 1)
            if t9 is not None:
                dve.wait_ge(s["c_lg"], t9 + 1)
                if due(t9):
                    dve.wait_ge(s["c_ex"], t9)
                dve.tensor_tensor(glog, b5[:, P:P + E], b_g, ALU.add).then_inc(s["c_lb"], 1)
                dve.wait_ge(s["c_lb"], t9 + 1)
                dve.tensor_reduce(gmax[:, 0:1], glog, AX.X, ALU.max, negate=True).then_inc(s["c_mx"], 1)
            if t0 is not None:
                stats("b0", tile(h, t0), pi, t0)

        dve.wait_ge(s["wf_in"], 16 * 20)
        for k in range(KD):
            dve.tensor_scalar(w_q[:, k, :], w_q[:, k, :], col[:, k:k + 1], None, ALU.mult)
            dve.tensor_scalar(w_down[:, k, :], w_down[:, k, :], col[:, k:k + 1], None, ALU.mult
                              ).then_inc(s["wf_s"], 1)
            dve.tensor_scalar(w_e[:, k, :], w_e[:, k, :], col[:, 2 + k:3 + k], None, ALU.mult)
            dve.tensor_scalar(w_g[:, k, :], w_g[:, k, :], col[:, 2 + k:3 + k], None, ALU.mult
                              ).then_inc(s["wf_s"], 1)
        skewed(dve, step_b, B, 11)

        def step_d(i, pi):
            normalise(i)
            heads(i, pi)
            t = at(i, 2)
            if t is not None:
                dve.wait_ge(s["d_qk"], t + 1)
                if due(t):
                    dve.wait_ge(s["d_qf"], t)
                qk = b3.rearrange("p (h d) -> p h d", d=HD)
                half = HD // 2
                dve.tensor_tensor(t1, qk, cosb.unsqueeze(1).to_broadcast([P, 2 * H, HD]), ALU.mult
                                  ).then_inc(s["d_rot"], 1)
                for lo, fro in ((0, half), (half, 0)):
                    dve.tensor_tensor(t2[:, :, lo:lo + half], qk[:, :, fro:fro + half],
                                      sinb[:, lo:lo + half].unsqueeze(1).to_broadcast([P, 2 * H, half]), ALU.mult
                                      ).then_inc(s["d_rot"], 1)
            t7 = at(i, 7)
            if t7 is not None:
                dve.wait_ge(s["h_Wo"], t7 + 1)
                dve.tensor_tensor(tile(h, t7), b2[:, 0:D], tile(h, t7), ALU.add).then_inc(s["h_upd"], 1)
            t = at(i, 1)
            if t is not None:
                rs_ready("d0", t)
                if due(t - 1):
                    dve.wait_ge(s["d_T"], t - 1)
                normed(xn[(pi - 1) % 2], tile(h, t), 0, (pi - 1) % 2, "d_xn")
            t = at(i, 3)
            if t is not None:
                low(t, (pi - 3) % 2)
            t = at(i, 9)
            if t is not None:
                u = (pi - 9) % 2
                rs_ready("e1", t)
                if due(t - 1):
                    dve.wait_ge(s["e_T"], t - 1)
                if due(8 * (t - u)):
                    dve.wait_ge(s[f"e_xout{u}"], 8 * (t - u))
                normed(en[u], tile(h, t), 1, u, "e_xn")
            t = at(i, 8)
            if t is not None:
                count = ready(dve, t + 1)
                dve.wait_ge(s["small_in"], 16 * 8)
                dve.wait_ge(s["h_upd"], count)
                stats("e1", tile(h, t), pi % 2, t)
            t = at(i, 0)
            if t is not None:
                stats("d0", tile(h, t), pi, t)

        skewed(dve, step_d, B, 10)

        done = [0]

        def chain(ins):
            done[0] += 1
            ins.then_inc(s["r_dve"], 1)
            if due(done[0]):
                dve.wait_ge(s["r_dve"], done[0])

        def c_(name):
            lo, n = CST[name]
            return cst[:, lo:lo + n]

        dve.wait_ge(s["e_lgs"], B)
        chain(dve.tensor_reduce(r_max, LG[:], AX.X, ALU.max))
        chain(dve.tensor_tensor(r_tmp, LG[:], r_max.unsqueeze(2).to_broadcast([P, B, E]), ALU.is_ge))
        chain(dve.tensor_tensor(r_tmp, r_tmp, c_("rank").unsqueeze(1).to_broadcast([P, B, E]), ALU.mult))
        chain(dve.tensor_reduce(r_max, r_tmp, AX.X, ALU.max))
        chain(dve.tensor_tensor(r_hot, r_tmp, r_max.unsqueeze(2).to_broadcast([P, B, E]), ALU.is_equal))
        chain(dve.tensor_copy(r_hot_b, r_hot))
        dve.wait_ge(s["r_pe"], 1)
        chain(dve.tensor_tensor(r_cmp, b1[:, 0:E].unsqueeze(2).to_broadcast([P, E, B]),
                                c_("tiles").unsqueeze(1).to_broadcast([P, E, B]), ALU.is_gt))
        chain(dve.tensor_reduce(r_n, r_cmp, AX.X, ALU.add))
        chain(dve.tensor_copy(r_ci, r_n))
        for e in range(1, E):
            chain(dve.tensor_tensor(r_ci[:, e:e + 1], r_ci[:, e - 1:e], r_n[:, e:e + 1], ALU.add))
        chain(dve.tensor_tensor(r_base, r_ci, r_n, ALU.subtract))
        chain(dve.tensor_scalar(r_base, r_base, float(P), None, ALU.mult))
        chain(dve.tensor_tensor(r_tmp, b0[:, 0:B * E].rearrange("p (b e) -> p b e", b=B),
                                r_base.unsqueeze(1).to_broadcast([P, B, E]), ALU.add))
        chain(dve.tensor_tensor(r_tmp, r_tmp, r_hot, ALU.mult))
        chain(dve.tensor_reduce(r_slot, r_tmp, AX.X, ALU.add))
        chain(dve.tensor_copy(r_slot_i, r_slot))
        chain(dve.tensor_scalar(r_a_i, r_slot_i, 7, None, ALU.logical_shift_right))
        chain(dve.tensor_scalar(r_b_i, r_slot_i, P - 1, None, ALU.bitwise_and))
        chain(dve.tensor_copy(r_a, r_a_i))
        chain(dve.tensor_copy(r_b, r_b_i))
        chain(dve.tensor_tensor(r_hot_a, r_a.unsqueeze(2).to_broadcast([P, B, NJ]),
                                c_("slot_tile").unsqueeze(1).to_broadcast([P, B, NJ]), ALU.is_equal))
        chain(dve.tensor_tensor(r_hot_a, r_hot_a, c_("token").unsqueeze(2).to_broadcast([P, B, NJ]), ALU.mult))
        dve.tensor_tensor(r_hot_c, r_b.unsqueeze(2).to_broadcast([P, B, P]),
                          c_("place").unsqueeze(1).to_broadcast([P, B, P]), ALU.is_equal).then_inc(s["r_hots"], 1)
        chain(dve.tensor_tensor(r_te, c_("slot_tile").unsqueeze(2).to_broadcast([P, NJ, E]),
                                r_ci.unsqueeze(1).to_broadcast([P, NJ, E]), ALU.is_ge))
        chain(dve.tensor_reduce(r_tile, r_te, AX.X, ALU.add))
        chain(dve.tensor_scalar(texp_i[:], r_tile, float(E - 1), None, ALU.min))
        dve.wait_ge(s["r_pe"], 2)
        chain(dve.tensor_copy(r_id, b2[:, 0:NJ]))
        chain(dve.tensor_scalar(r_far, r_id, 0.0, FAR, ALU.is_equal, ALU.mult))
        chain(dve.tensor_scalar(r_idg, r_id, -1.0, 0.0, ALU.add, ALU.max))
        chain(dve.tensor_copy(idx_i[:, 0, :], r_idg))
        chain(dve.tensor_tensor(idx_i[:, 1, :], r_idg, r_far, ALU.add))
        dve.sem_inc(s["r_tables"], 1)

        def step_f(i, pi):
            j = at(i, 4, NJ)
            if j is not None:
                u = pi % 2
                dve.wait_ge(s["f_down"], j + 1)
                dve.wait_ge(s[f"f_hin{u}"], 8 * (j - u) + 16)
                if due(8 * (j - u)):
                    dve.wait_ge(s[f"f_out{u}"], 8 * (j - u))
                dve.tensor_tensor(yo[u], b7[:, 0:D], gh[u], ALU.add).then_inc(s["f_y"], 1)
            j = at(i, 2, NJ)
            if j is not None:
                u = pi % 2
                dve.wait_ge(s["f_up"], j + 1)
                dve.wait_ge(s["f_silu"], j + 1)
                if due(j - 1):
                    dve.wait_ge(s["f_Tb"], j - 1)
                dve.tensor_tensor(hm[u].rearrange("p (n i) -> p n i", n=2), PS[:, 3:5, 0:IH],
                                  sg.rearrange("p (n i) -> p n i", n=2), ALU.mult).then_inc(s["f_hm"], 1)
            j = at(i, 3, NJ)
            if j is not None:
                u = (pi - 3) % 2
                dve.wait_ge(s["f_Tb"], j + 1)
                if due(j - 1):
                    dve.wait_ge(s["f_down"], j - 1)
                dve.tensor_copy(hT[u][:, 3:5, :].rearrange("p k t -> p (k t)"), b6[:, 0:2 * P])
                dve.tensor_copy(hT[u][0:IR, 5, :], b6[0:IR, 2 * P:3 * P]).then_inc(s["f_hTb"], 1)
            j = at(i, 1, NJ)
            if j is not None:
                u = (pi - 1) % 2
                dve.wait_ge(s["f_T"], j + 1)
                if due(j - 1):
                    dve.wait_ge(s["f_up"], j - 1)
                dve.tensor_copy(xsT[u].rearrange("p k t -> p (k t)"), b0[:, 0:D]).then_inc(s["f_xT"], 1)

        skewed(dve, step_f, NJ, 5)


CST = {"rank": (0, E), "tiles": (E, B), "slot_tile": (E + B, NJ), "token": (E + B + NJ, B),
       "place": (E + 2 * B + NJ, P)}


def constants():
    wide = E + 2 * B + NJ + P
    c = np.zeros((P, wide), np.float32)

    def put(name, v):
        lo, n = CST[name]
        c[:, lo:lo + n] = v

    put("rank", E - np.arange(E))
    put("tiles", P * np.arange(B))
    put("slot_tile", np.arange(NJ))
    put("token", P * np.arange(B)[None, :] + np.arange(P)[:, None] + 1)
    put("place", np.arange(P))
    inv = (1.0 / 10000.0 ** (np.arange(0, HD, 2, dtype=np.float32) / HD)).astype(np.float32)
    f = np.outer(np.arange(P, dtype=np.float32), inv).astype(np.float32)
    cos = np.concatenate([np.cos(f), np.cos(f)], 1).astype(np.float32)
    sin = np.concatenate([-np.sin(f), np.sin(f)], 1).astype(np.float32)
    return {"cst": c, "cos": cos, "sin": sin, "ident": np.eye(P, dtype=np.float32)}


def kernel(**inputs):
    import concourse.bacc as bacc
    from concourse.bass_utils import run_bass_kernel_spmd

    a = {k: np.asarray(v) for k, v in inputs.items()}

    def plain(x):
        return np.ascontiguousarray(x)

    arrays = {k: plain(a[k]) for k in (
        "L0_tok_word_emb L0_tok_pos_emb L0_tok_type_emb L0_tok_gamma L0_tok_beta L0_ffn_Wq L0_ffn_bq L0_ffn_Wdown "
        "L0_ffn_Wup L0_ffn_bup L0_ffn_Wo L0_ffn_bo L0_ffn_Wg L0_ffn_bg L0_ffn_We").split()}
    for k in "L0_attn_wq L0_attn_wk L0_attn_wv L1_attn_Wq L1_attn_Wk L1_attn_Wv L1_attn_Wo".split():
        arrays[k + "T"] = plain(a[k].T)
    arrays["idsT"] = plain(a["x"].T)
    arrays["typesT"] = plain(a["mask_BS_i1_0"].T)
    arrays["gamma1T"] = plain(a["L0_ffn_gamma1"].reshape(KD, P).T)
    arrays["gamma2T"] = plain(a["L0_ffn_gamma2"].reshape(KD, P).T)
    arrays["bdownT"] = plain(a["L0_ffn_bdown"].reshape(LAT, 1))
    arrays["routerT"] = plain(a["L1_ffn_router_w"].T)
    arrays["gateT"] = plain(a["L1_ffn_gate_w"].transpose(0, 2, 1))
    arrays["upT"] = plain(a["L1_ffn_up_w"].transpose(0, 2, 1))
    arrays["downT"] = plain(a["L1_ffn_down_w"].transpose(0, 2, 1))
    arrays.update(constants())

    nc = bacc.Bacc("TRN2", target_bir_lowering=False, num_devices=1)
    dr = {k: nc.dram_tensor(f"in_{k}", v.shape, mybir.dt.from_np(v.dtype), kind="ExternalInput").ap()
          for k, v in arrays.items()}
    dr["out"] = nc.dram_tensor("out", (B * P, D), F32, kind="ExternalOutput").ap()
    build(nc, dr)
    r = run_bass_kernel_spmd(nc, [{f"in_{k}": v for k, v in arrays.items()}], core_ids=[0])
    return r.results[0]["out"].reshape(B, P, D)
```

```python
from contextlib import ExitStack

import numpy as np

import concourse.bass as bass
from concourse import mybir

F32 = mybir.dt.float32
F32R = mybir.dt.float32r
BF16 = mybir.dt.bfloat16
I32 = mybir.dt.int32
U32 = mybir.dt.uint32
ALU = mybir.AluOpType
ACT = mybir.ActivationFunctionType
AX = mybir.AxisListType

P = 128
B = 16
D = 256
KD = D // P
H = 16
HD = D // H
NB = H // 2
PART = 3 * HD
AUG = PART + 2
LAT = 64
E = 8
I = 704
IH = I // 2
KI = (I + P - 1) // P
IR = I - (KI - 1) * P
GU = KD * 2 * I
WE = GU + KI * D
NJ = B + E - 1
HP = 5
NEG = -3.0e38
SCALE0 = float(P) ** -0.5
SCALEH = float(HD) ** -0.5
FAR = 8192.0

SEMAPHORES = (
    "small_in ids_in w0_in wf_in w1_in rows_in rows_mid rows_late experts_in "
    "p_set masks ident_b prep wa_ps wa wv_mx wv_ex wv_ri wv_s wf_s "
    "n0_st n0_ag n0_ep n0_rs n1_st n1_ag n1_ep n1_rs n2_ag n2_ep n2_rs "
    "a_x a_xt a_ng a_h a_xn a_T a_xT a_u a_v a_uT a_vs a_S a_mr a_mx a_E a_ri a_vn a_O a_done "
    "b_x2 b_xn b_T b_xT b_q b_c b_cT b_kv b_kf b_qf b_vf "
    "g_qk_mul g_S g_max g_sub g_exp g_sum g_ri g_pv_pool g_pv_dve g_O g_o g_oT g_oTs g_Wo g_upd "
    "c_xn c_T c_xT c_lg c_lb c_mx c_ex c_ri c_gt c_exp c_es c_sum c_acc "
    "d_xn d_T d_xT d_qk d_v d_rot d_qf d_vf "
    "e_xn e_T e_xT e_lg e_lgs e_hout e_xout0 e_xout1 "
    "h_hi h_dup h_lo h_padT h_qkT h_S1 h_max h_nh h_nl h_nT h_nTs h_aug h_S2 h_exp h_va h_AV h_OTs "
    "h_OTT h_ri h_o h_oT h_oTs h_Wo h_upd "
    "r_pe r_dve r_hots r_tables "
    "f_warm f_gi f_xin0 f_xin1 f_T f_xT f_gate f_up f_silu f_hm f_Ta f_Tb f_hTa f_hTb f_down f_hi f_hin0 f_hin1 f_y "
    "f_si f_out0 f_out1"
).split()

NORMS = {"a0": (0, 0), "b0": (0, B), "d0": (0, 2 * B), "a1": (1, 0), "b1": (1, B), "e1": (1, 2 * B), "c0": (2, 0)}
TAKEN = {"a0": 0, "b0": B, "d0": 2 * B, "a1": 0, "e1": B}


def rows(ap, k):
    return ap.rearrange("(k p) n -> p k n", k=k)


def build(nc, dr):
    with ExitStack() as ctx:
        program(nc, dr, ctx)


def program(nc, dr, ctx):
    def sb(name, shape, dt=F32):
        return ctx.enter_context(nc.sbuf_tensor(name, shape, dt))

    s = {name: ctx.enter_context(nc.semaphore(name)) for name in SEMAPHORES}

    def due(n):
        return not isinstance(n, int) or n > 0

    def ready(eng, n):
        return n if isinstance(n, int) else eng.to_reg(n)

    W = sb("W", [P, E, WE])
    h = sb("h", [P, B, D])
    v_all = sb("v_all", [P, B * D])
    pad = sb("pad", [P, 2, H, 64], F32R)
    qT = [sb(f"qT{u}", [P, NB, P], F32R) for u in range(2)]
    kT = [[sb(f"kT{u}_{f}", [P, NB, P], F32R) for f in range(2)] for u in range(2)]
    nms = sb("nms", [P, P], F32R)
    nmT = sb("nmT", [32, P], F32R)
    ident = sb("ident", [P, P])
    ident_b = sb("ident_b", [P, P], BF16)
    mask_qk = sb("mask_qk", [P, P], BF16)
    mask_kq = sb("mask_kq", [P, P], BF16)
    before = sb("before", [P, P], BF16)
    ones_b = sb("ones_b", [P, P], BF16)
    neghalf = sb("neghalf", [P, 1])
    w_router = sb("w_router", [P, KD, E])
    stat = [sb(f"stat{u}", [P, 6]) for u in range(3)]
    mv = [[sb(f"mv{n}_{u}", [P, 2]) for u in range(2)] for n in range(3)]
    rs = [[sb(f"rs{n}_{u}", [P, 2]) for u in range(2)] for n in range(3)]
    nmax = sb("nmax", [P, H])
    rinv = sb("rinv", [P, H])
    LG = sb("LG", [P, B, E])
    idx_i = sb("idx_i", [P, 2, NJ], I32)
    texp_i = sb("texp_i", [P, NJ], I32)
    gi = [sb(f"gi{u}", [P, 1], I32) for u in range(2)]
    hi_ = [sb(f"hi{u}", [P, 1], I32) for u in range(2)]
    si = [sb(f"si{u}", [P, 1], I32) for u in range(2)]
    ids = sb("ids", [P, B], I32)
    typ_i = sb("typ_i", [P, B], I32)
    cst = sb("cst", [P, E + B + NJ + 1 + P])
    v_tiles = v_all[:].rearrange("p (b d) -> p b d", b=B)
    t01 = v_all[:, 0:2 * D].rearrange("p (a d) -> p a d", a=2)

    first = {0: 0, 2: 0, 5: 0}

    def carve(e0, shape, parts=P):
        n = int(np.prod(shape))
        at = first[e0]
        first[e0] = at + n
        count = 3 if e0 else 2
        assert first[e0] <= count * WE, first
        flat = W[:, e0:e0 + count, :].rearrange("p e w -> p (e w)")[0:parts, at:at + n]
        if len(shape) == 2:
            flat = flat.rearrange("p (a b) -> p a b", a=shape[0])
        if len(shape) == 3:
            flat = flat.rearrange("p (a b c) -> p a b c", a=shape[0], b=shape[1])
        return flat

    qk = carve(0, (H * H * HD,))
    pv = carve(0, (H * H * HD,))
    rsum = [carve(0, (H,)) for _ in range(2)]
    hmax = carve(0, (H,))
    w_e = carve(2, (KD, E * D))
    minus_ident = carve(0, (P,))
    x2 = carve(2, (B, D))
    wqT = carve(2, (KD, D))
    wkT = carve(2, (KD, D))
    w_a = carve(2, (KD, D))
    w_vs = carve(2, (KD, D))
    w_q = carve(2, (KD, D))
    w_down = carve(2, (KD, LAT))
    w_up = carve(2, (2 * D,), LAT)
    w_o0 = carve(2, (KD, D))
    w_g = carve(2, (KD, E))
    col = carve(2, (8,))
    b_g = carve(2, (E,))
    w_qk1 = carve(5, (KD, 2 * D))
    w_v1 = carve(5, (KD, D))
    w_o1 = carve(5, (KD, D))
    pos_t = carve(5, (D,))
    dtype_ = carve(5, (D,))
    gam = carve(5, (D,))
    bet = carve(5, (D,))
    b_q = carve(2, (D,))
    b_up = carve(2, (2 * D,))
    b_o = carve(2, (D,))
    cosb = carve(5, (HD,))
    sinb = carve(5, (HD,))
    typ = carve(5, (B,))
    wv_small = carve(5, (8,))
    n0 = carve(5, (D,))
    xn = [carve(5, (D,)) for _ in range(2)]
    xT = [carve(5, (KD, P)) for _ in range(2)]
    PT = carve(5, (H, P))
    ots = carve(5, (4 * P,))
    o_sb = carve(5, (D,))
    oT = carve(5, (KD, P))
    vaug = [carve(5, (H, 32)) for _ in range(2)]
    mark = first[5]
    cT = carve(5, (P,), LAT)
    qkf = [carve(5, (2, H, HD)) for _ in range(2)]
    rot_a = carve(5, (2 * H, HD))
    rot_b = carve(5, (2 * H, HD))
    first[5] = mark
    uT = [carve(5, (KD, P)) for _ in range(2)]
    va_ = [carve(5, (D,)) for _ in range(2)]
    ET = [carve(5, (P,)) for _ in range(2)]
    vn = carve(5, (D,))
    sm = [carve(5, (4,)) for _ in range(2)]
    first[5] = mark + P + 2 * 2 * H * HD
    sc = [carve(5, (H, H)) for _ in range(2)]
    gate = [carve(5, (E,)) for _ in range(2)]
    gsum = [carve(5, (2,)) for _ in range(2)]
    gmax = carve(5, (2,))
    glog = carve(5, (E,))
    es = PT.rearrange("p h t -> p (h t)").rearrange("p (e d) -> p e d", e=E)

    first[5] = max(first[5], mark + 3 * 512 * 2 + P)
    en = [carve(5, (D,)) for _ in range(2)]
    eT = [carve(5, (KD, P)) for _ in range(2)]

    free = [0]

    def table(shape, dt=F32):
        n = int(np.prod(shape))
        lo, free[0] = free[0], free[0] + (n + 1) // 2 * (1 if dt == BF16 else 2)
        hi = free[0]
        flat = v_all[:, lo:lo + n] if dt == F32 else v_all[:, lo:hi].bitcast(dt)[:, 0:n]
        assert hi <= B * D
        return flat.rearrange("p (a b) -> p a b", a=shape[0]) if len(shape) == 2 else \
            flat.rearrange("p (a b c) -> p a b c", a=shape[0], b=shape[1])

    r_hot = table((B, E))
    r_hot_b = table((B, E), BF16)
    r_tmp = table((B, E))
    r_max = table((1, B))[:, 0, :]
    r_n = table((1, E))[:, 0, :]
    r_ci = table((1, E))[:, 0, :]
    r_base = table((1, E))[:, 0, :]
    r_slot = table((1, B))[:, 0, :]
    r_slot_i = table((1, B), I32)[:, 0, :]
    r_a_i = table((1, B), I32)[:, 0, :]
    r_b_i = table((1, B), I32)[:, 0, :]
    r_a = table((1, B))[:, 0, :]
    r_b = table((1, B))[:, 0, :]
    r_cmp = table((E, B))
    r_te = table((NJ, E))
    r_tile = table((1, NJ))[:, 0, :]
    r_id = table((1, NJ))[:, 0, :]
    r_far = table((1, NJ))[:, 0, :]
    r_idg = table((1, NJ))[:, 0, :]
    r_hot_a = table((B, NJ))
    r_token = [table((B, NJ), BF16) for _ in range(2)]
    r_hot_c = table((B, P), BF16)
    sg = v_all[:, 0:I]
    hm = [v_all[:, I * (1 + u):I * (2 + u)] for u in range(2)]
    late = pad[:].rearrange("p a h c -> p (a h c)").bitcast(F32)
    gx = [late[:, D * u:D * (u + 1)] for u in range(2)]
    xsT = [late[:, D * (2 + u):D * (3 + u)].rearrange("p (k t) -> p k t", k=KD) for u in range(2)]
    hT = [v_all[:, 3 * I:3 * I + KI * P].rearrange("p (k t) -> p k t", k=KI),
          late[:, 4 * D:4 * D + KI * P].rearrange("p (k t) -> p k t", k=KI)]

    lo = 3 * I + KI * P
    gh = [v_all[:, lo + D * u:lo + D * (u + 1)] for u in range(2)]
    yo = [v_all[:, lo + D * (2 + u):lo + D * (3 + u)] for u in range(2)]

    PS = ctx.enter_context(nc.psum_tensor("PS", [P, 8, 512], F32))
    b0, b1, b2, b3, b4, b5, b6, b7 = (PS[:, n, :] for n in range(8))

    h_dram = nc.dram_tensor("h_rows", [B * P, D], F32).ap()
    xn_dram = nc.dram_tensor("xn_rows", [B * P, D], F32).ap()
    out = dr["out"]

    block = ctx.enter_context(nc.Block())

    def skewed(eng, step, n, depth):
        head = depth + 2 - depth % 2
        tail = head + (n - head) // 2 * 2
        for i in range(head):
            step(i, i % 2)
        with eng.Fori(head // 2, tail // 2) as m:
            step(2 * m, 0)
            step(2 * m + 1, 1)
        for i in range(tail, n + depth - 1):
            step(i, i % 2)

    def at(i, k, n=B):
        if isinstance(i, int):
            return i - k if 0 <= i - k < n else None
        return i - k if k else i

    def done(i, k):
        return min(max(i - k + 1, 0), B) if isinstance(i, int) else i - k + 1

    def tile(x, t):
        if isinstance(t, int):
            return x[:, t]
        return x[:, bass.ds(t, 1)].rearrange("p a d -> p (a d)")

    def over_heads(ap):
        return ap.rearrange("p (h d) -> p h d", h=H)

    def heads3(x):
        return x.rearrange("p (h a b) -> p h a b", h=H, a=H)

    def over_keys(p_):
        return p_.unsqueeze(2).to_broadcast([P, p_.shape[1], HD, H])

    def over_queries(v, n):
        return v.rearrange("p (g d) -> p d g", g=H).unsqueeze(1).to_broadcast([P, n, HD, H])

    o_heads = over_heads(o_sb)

    def qk_out(eng, t, u, r, half=None):
        eng.wait_ge(s["h_padT"], 4 * t + r + 1)
        read = 4 * (t - 2) + 3 + r % 2
        if due(read):
            eng.wait_ge(s["h_S2"], read)
        rows_, to = (slice(0, P), qT[u]) if half is None else (slice(64 * half, 64 * half + 64), kT[u][half])
        dst = to[rows_, 4 * (r % 2):4 * (r % 2) + 4, :].rearrange("p b t -> p (b t)")
        if eng is nc.scalar:
            nc.scalar.activation(dst, b0[rows_], ACT.Copy).then_inc(s["h_qkT"], 1)
        else:
            nc.vector.tensor_copy(dst, b0[rows_]).then_inc(s["h_qkT"], 1)

    @block.sync
    def _(sp):
        def load(dst, src, sem):
            sp.dma_start(dst, src).then_inc(s[sem], 16)

        load(ids[:], dr["idsT"], "ids_in")
        load(wqT, rows(dr["L0_attn_wqT"], KD), "w0_in")
        load(wkT, rows(dr["L0_attn_wkT"], KD), "w0_in")
        load(w_vs, rows(dr["L0_attn_wvT"], KD), "w0_in")
        load(typ_i[:], dr["typesT"], "small_in")
        load(pos_t, dr["L0_tok_pos_emb"], "small_in")
        load(t01[:, 0, :], dr["L0_tok_type_emb"][0, :].partition_broadcast(P), "small_in")
        load(t01[:, 1, :], dr["L0_tok_type_emb"][1, :].partition_broadcast(P), "small_in")
        load(gam, dr["L0_tok_gamma"].partition_broadcast(P), "small_in")
        load(bet, dr["L0_tok_beta"].partition_broadcast(P), "small_in")
        load(ident[:], dr["ident"], "small_in")
        load(cst[:], dr["cst"], "small_in")
        load(w_q, rows(dr["L0_ffn_Wq"], KD), "wf_in")
        load(w_down, rows(dr["L0_ffn_Wdown"], KD), "wf_in")
        load(w_up, dr["L0_ffn_Wup"], "wf_in")
        load(w_o0, rows(dr["L0_ffn_Wo"], KD), "wf_in")
        load(w_g, rows(dr["L0_ffn_Wg"], KD), "wf_in")
        load(col[:, 0:2], dr["gamma1T"], "wf_in")
        load(col[:, 2:4], dr["gamma2T"], "wf_in")
        load(col[0:LAT, 4:5], dr["bdownT"], "wf_in")
        load(b_q, dr["L0_ffn_bq"].partition_broadcast(P), "wf_in")
        load(b_up, dr["L0_ffn_bup"].partition_broadcast(P), "wf_in")
        load(b_o, dr["L0_ffn_bo"].partition_broadcast(P), "wf_in")
        load(b_g, dr["L0_ffn_bg"].partition_broadcast(P), "wf_in")
        for e in range(E):
            load(w_e[:, :, e * D:(e + 1) * D], rows(dr["L0_ffn_We"][e], KD), "wf_in")
        load(w_qk1[:, :, 0:D], rows(dr["L1_attn_WqT"], KD), "w1_in")
        load(w_qk1[:, :, D:2 * D], rows(dr["L1_attn_WkT"], KD), "w1_in")
        load(w_v1, rows(dr["L1_attn_WvT"], KD), "w1_in")
        load(w_o1, rows(dr["L1_attn_WoT"], KD), "w1_in")
        load(w_router[:], rows(dr["routerT"], KD), "w1_in")
        load(cosb, dr["cos"], "w1_in")
        load(sinb, dr["sin"], "w1_in")

        def load_expert(e):
            gu = W[:, e, 0:GU].rearrange("p (k g i) -> p k g i", k=KD, g=2)
            load(gu[:, :, 0, :], rows(dr["gateT"][e], KD), "experts_in")
            load(gu[:, :, 1, :], rows(dr["upT"][e], KD), "experts_in")
            wd = W[:, e, GU:WE].rearrange("p (k d) -> p k d", k=KI)
            load(wd[:, 0:KI - 1, :], rows(dr["downT"][e, 0:(KI - 1) * P, :], KI - 1), "experts_in")
            load(wd[0:IR, KI - 1, :], dr["downT"][e, (KI - 1) * P:I, :], "experts_in")

        def maxima_into_q(t, u):
            sp.wait_ge(s["h_nTs"], t + 1)
            for f in range(2):
                for a in range(2):
                    r = NB * (2 * f + a)
                    row = 64 * f + PART + a
                    sp.dma_start(qT[u][row:row + 1, :, :].bitcast(F32), nmT[r:r + NB, :].bitcast(F32)
                                 ).then_inc(s["h_aug"], 16)

        sp.wait_ge(s["c_acc"], B)
        for e in range(5):
            load_expert(e)

        def step_d(i, pi):
            t = at(i, 5)
            if t is not None:
                maxima_into_q(t, (pi - 5) % 2)
            t = at(i, 9)
            if t is not None:
                u = (pi - 9) % 2
                sp.wait_ge(s["e_xn"], t + 1)
                lo = t * P
                sp.dma_start(xn_dram[bass.ds(lo, P), :], en[u]).then_inc(s[f"e_xout{u}"], 16)
                sp.dma_start(h_dram[bass.ds(lo, P), :], tile(h, t)).then_inc(s["e_hout"], 16)

        skewed(sp, step_d, B, 10)
        sp.wait_ge(s["e_lgs"], B)
        sp.wait_ge(s["h_upd"], B)
        sp.wait_ge(s["e_xout0"], 8 * B)
        sp.wait_ge(s["e_xout1"], 8 * B)
        for e in range(5, 8):
            load_expert(e)

    @block.gpsimd
    def _(pool):
        pool.memset(neghalf[:], -0.5).then_inc(s["p_set"], 1)

        def gather(t, name):
            pool.indirect_dma_start(h[:, t, :], None, dr["L0_tok_word_emb"],
                                    bass.IndirectOffsetOnAxis(ap=ids[:, t:t + 1], axis=0)).then_inc(s[name], 16)

        pool.wait_ge(s["ids_in"], 16)
        for t in range(4):
            gather(t, "rows_in")

        def rstd(x, u, t, eps):
            n, base = NORMS[x]
            count = ready(pool, base + t + 1)
            pool.wait_ge(s["p_set"], 1)
            pool.wait_ge(s[f"n{n}_ag"], count)
            pool.tensor_scalar(rs[n][u][:, 0:1], mv[n][u][:, 1:2], eps, None, ALU.add).then_inc(s[f"n{n}_ep"], 1)
            power(n, base + t, u)

        def rrms(x, u, t, eps):
            n, base = NORMS[x]
            count = ready(pool, base + t + 1)
            pool.wait_ge(s["p_set"], 1)
            pool.wait_ge(s[f"n{n}_ag"], count)
            pool.tensor_scalar(rs[n][u][:, 0:1], mv[n][u][:, 0:1], 1.0 / D, eps, ALU.mult, ALU.add
                               ).then_inc(s[f"n{n}_ep"], 1)
            power(n, base + t, u)

        def power(n, done, u):
            pool.wait_ge(s[f"n{n}_ep"], done + 1)
            pool.tensor_tensor(rs[n][u][:, 1:2], rs[n][u][:, 0:1], neghalf[:], ALU.pow).then_inc(s[f"n{n}_rs"], 1)

        def step_a(i, pi):
            t0, t1_, t2 = at(i, 0), at(i, 1), at(i, 2)
            if isinstance(i, int) and i < 6:
                for t in (4 + 2 * i, 5 + 2 * i):
                    gather(t, "rows_mid" if t < 8 else "rows_late")
            if t0 is not None:
                if isinstance(i, int) and i in (0, 4):
                    pool.wait_ge(s["rows_in" if i == 0 else "rows_mid"], 16 * 4)
                pool.tensor_tensor(tile(h, t0), tile(h, t0), pos_t, ALU.add).then_inc(s["a_x"], 1)
            if t1_ is not None:
                rstd("a0", (pi - 1) % 2, t1_, 1e-12)
            if t2 is not None:
                rstd("a1", pi % 2, t2, 1e-5)
            if isinstance(i, int) and i == 7:
                pool.wait_ge(s["rows_late"], 16 * (B - 8))

        def dup(t):
            count = ready(pool, t + 1)
            pool.wait_ge(s["p_set"], 1)
            pool.wait_ge(s["h_hi"], count)
            pool.tensor_copy(pad[:, 0, :, 2 * HD:3 * HD], pad[:, 0, :, 0:HD]).then_inc(s["h_dup"], 1)
            pool.tensor_copy(pad[:, 1, :, HD:2 * HD], pad[:, 1, :, 0:HD]).then_inc(s["h_dup"], 1)

        def values(t, u):
            pool.wait_ge(s["d_vf"], t + 1)
            if due(t - 1):
                pool.wait_ge(s["h_AV"], t - 1)
            pool.tensor_copy(vaug[u][:, :, 0:HD], tile(v_tiles, t).rearrange("p (h d) -> p h d", h=H)
                             ).then_inc(s["h_va"], 1)

        def step_b(i, pi):
            t = at(i, 6)
            if t is not None:
                u = pi % 2
                pool.wait_ge(s["g_exp"], t + 1)
                if due(2 * t):
                    pool.wait_ge(s["g_O"], 2 * t)
                pool.tensor_tensor(heads3(pv)[:, 0:HP], over_keys(sc[u][:, 0:HP]), over_queries(tile(v_tiles, t), HP),
                                   ALU.mult).then_inc(s["g_pv_pool"], 1)
            t = at(i, 4)
            if t is not None:
                u = pi % 2
                pool.wait_ge(s["b_qf"], t + 1)
                pool.wait_ge(s["b_kf"], t + 1)
                for g in range(4):
                    if due(4 * (t - 1) + g + 1):
                        pool.wait_ge(s["g_S"], 4 * (t - 1) + g + 1)
                    pool.tensor_tensor(heads3(qk)[:, 4 * g:4 * g + 4],
                                       qkf[u][:, 0, 4 * g:4 * g + 4].unsqueeze(2).to_broadcast([P, 4, H, HD]),
                                       qkf[u][:, 1].unsqueeze(1).to_broadcast([P, 4, H, HD]), ALU.mult
                                       ).then_inc(s["g_qk_mul"], 1)
            t = at(i, 8)
            if t is not None:
                rrms("c0", pi % 2, t, 1e-6)
            t = at(i, 1)
            if t is not None:
                rrms("b1", (pi - 1) % 2, t, 1e-6)
            t = at(i, 0)
            if t is not None:
                rstd("b0", pi, t, 1e-5)

        def step_d(i, pi):
            t0, t2, t3, t5, t8 = (at(i, k) for k in (0, 2, 3, 5, 8))
            if t5 is not None:
                values(t5, (pi - 5) % 2)
            if t2 is not None:
                u = pi % 2
                pool.wait_ge(s["d_rot"], 3 * t2 + 3)
                if due(t2 - 1):
                    pool.wait_ge(s["h_lo"], 2 * (t2 - 1))
                    pool.wait_ge(s["h_hi"], t2 - 1)
                pool.tensor_tensor(qkf[u].rearrange("p a h d -> p (a h d)"), rot_a.rearrange("p h d -> p (h d)"),
                                   rot_b.rearrange("p h d -> p (h d)"), ALU.add).then_inc(s["d_qf"], 1)
            if t0 is not None:
                rstd("d0", pi, t0, 1e-5)
            if t8 is not None:
                rstd("e1", pi % 2, t8, 1e-5)
            if t3 is not None:
                dup(t3)

        pool.wait_ge(s["prep"], 4)
        skewed(pool, step_a, B, 7)
        pool.wait_ge(s["a_done"], B)
        skewed(pool, step_b, B, 11)

        pool.memset(nms[:].bitcast(F32), 0.0).then_inc(s["p_set"], 1)
        for u in range(2):
            for f in range(2):
                pool.memset(kT[u][f][:].bitcast(F32), 0.0).then_inc(s["p_set"], 1)
        pool.memset(pad[:].bitcast(F32), 0.0).then_inc(s["p_set"], 1)
        for u in range(2):
            pool.memset(vaug[u], 0.0).then_inc(s["p_set"], 1)
        pool.memset(mask_qk[:], 0.0).then_inc(s["p_set"], 1)
        pool.memset(mask_kq[:], 0.0).then_inc(s["p_set"], 1)
        pool.memset(before[:], 1.0).then_inc(s["p_set"], 1)
        pool.memset(ones_b[:], 1.0).then_inc(s["p_set"], 1)
        pool.wait_ge(s["p_set"], 13)
        pool.memset(pad[:, 1, :, PART:AUG].bitcast(F32), 1.0).then_inc(s["masks"], 1)
        for u in range(2):
            pool.memset(vaug[u][:, :, HD:HD + 1], 1.0).then_inc(s["masks"], 1)
        pool.affine_select(out=mask_qk[:], in_=mask_qk[:], compare_op=ALU.is_ge, fill=NEG, base=0,
                           pattern=[[-1, P]], channel_multiplier=1).then_inc(s["masks"], 1)
        pool.affine_select(out=mask_kq[:], in_=mask_kq[:], compare_op=ALU.is_ge, fill=NEG, base=0,
                           pattern=[[1, P]], channel_multiplier=-1).then_inc(s["masks"], 1)
        pool.affine_select(out=before[:], in_=before[:], compare_op=ALU.is_gt, fill=0.0, base=0,
                           pattern=[[1, P]], channel_multiplier=-1).then_inc(s["masks"], 1)
        pool.wait_ge(s["c_acc"], B)
        skewed(pool, step_d, B, 10)

        def index(dst, row, j, name):
            pool.tensor_copy(dst, idx_i[:, row, bass.ds(j, 1)]).then_inc(s[name], 1)
            count = ready(pool, j + 1)
            pool.wait_ge(s["r_tables"], 1)
            pool.wait_ge(s[name], count)

        def step_f(i, pi):
            j = at(i, 4, NJ)
            if j is not None:
                u = pi % 2
                if due(8 * (j - u)):
                    pool.wait_ge(s[f"f_out{u}"], 8 * (j - u))
                index(si[u][:], 1, j, "f_si")
                count = ready(pool, j + 1)
                pool.wait_ge(s["r_tables"], 1)
                pool.wait_ge(s["f_y"], count)
                pool.indirect_dma_start(out, bass.IndirectOffsetOnAxis(ap=si[u][:], axis=0), yo[u], None,
                                        bounds_check=B * P - 1, oob_is_err=False).then_inc(s[f"f_out{u}"], 16)
            j = at(i, 3, NJ)
            if j is not None:
                u = (pi - 3) % 2
                if due(8 * (j - u)):
                    pool.wait_ge(s[f"f_hin{u}"], 8 * (j - u))
                index(hi_[u][:], 0, j, "f_hi")
                if due(j - 1):
                    count = ready(pool, j - 1)
                    pool.wait_ge(s["r_tables"], 1)
                    pool.wait_ge(s["f_y"], count)
                pool.indirect_dma_start(gh[u], None, h_dram, bass.IndirectOffsetOnAxis(ap=hi_[u][:], axis=0)
                                        ).then_inc(s[f"f_hin{u}"], 16)
            j = at(i, 0, NJ)
            if j is not None:
                u = pi
                if due(8 * (j - u)):
                    pool.wait_ge(s[f"f_xin{u}"], 8 * (j - u))
                index(gi[u][:], 0, j, "f_gi")
                if due(j - 1):
                    count = ready(pool, j - 1)
                    pool.wait_ge(s["r_tables"], 1)
                    pool.wait_ge(s["f_T"], count)
                pool.indirect_dma_start(gx[u], None, xn_dram, bass.IndirectOffsetOnAxis(ap=gi[u][:], axis=0)
                                        ).then_inc(s[f"f_xin{u}"], 16)

        pool.wait_ge(s["r_tables"], 1)
        pool.wait_ge(s["e_xout0"], 8 * B)
        pool.wait_ge(s["e_xout1"], 8 * B)
        pool.wait_ge(s["e_hout"], 16 * B)
        skewed(pool, step_f, NJ, 5)
        pool.wait_ge(s["f_out0"], 16 * ((NJ + 1) // 2))
        pool.wait_ge(s["f_out1"], 16 * (NJ // 2))

    @block.tensor
    def _(pe):
        def transpose(dst, src, k, sem, count=1):
            for n in range(k):
                ins = pe.transpose(dst[:, n * P:(n + 1) * P], src[:, n * P:(n + 1) * P], ident[:])
            ins.then_inc(s[sem], 1)

        def product(dst, lhsT, rhs, sem):
            for n, (a, b) in enumerate(zip(lhsT, rhs)):
                ins = pe.matmul(dst, a, b, start=n == 0, stop=n == len(lhsT) - 1)
            if sem:
                ins.then_inc(s[sem], 1)

        def kt(x, lo=0, hi=None):
            return [x[:, k, lo:hi if hi else x.shape[2]] for k in range(x.shape[1])]

        pe.wait_ge(s["w0_in"], 48)
        for c in range(KD):
            product(PS[:, c, 0:D], kt(wqT, c * P, (c + 1) * P), kt(wkT), "wa_ps")

        def step_a(i, pi):
            t3, t4, t5, t6 = (at(i, k) for k in (3, 4, 5, 6))
            if t6 is not None:
                u = pi % 2
                pe.wait_ge(s["a_vn"], t6 + 1)
                if due(t6):
                    pe.wait_ge(s["a_done"], t6)
                pe.matmul(b4[:, 0:D], ident[:], tile(h, t6), start=True, stop=False)
                pe.matmul(b4[:, 0:D], minus_ident, va_[u], start=False, stop=False)
                pe.matmul(b4[:, 0:D], ET[u], vn, start=False, stop=True).then_inc(s["a_O"], 1)
            if t5 is not None:
                u = (pi - 5) % 2
                pe.wait_ge(s["a_uT"], t5 + 1)
                if due(t5):
                    pe.wait_ge(s["a_E"], t5)
                product(b1[:, 0:P], kt(xT[u]), kt(uT[u]), "a_S")
            if t4 is not None:
                u = pi % 2
                pe.wait_ge(s["a_xT"], t4 + 1)
                if due(t4):
                    pe.wait_ge(s["a_uT"], t4)
                for d in range(KD):
                    product(b3[:, d * P:(d + 1) * P], kt(w_a, d * P, (d + 1) * P), kt(xT[u]),
                            "a_u" if d == KD - 1 else None)
                if due(t4):
                    pe.wait_ge(s["a_vs"], t4)
                product(b7[:, 0:D], kt(xT[u]), kt(w_vs), "a_v")
            if t3 is not None:
                pe.wait_ge(s["a_xn"], t3 + 1)
                if due(t3):
                    pe.wait_ge(s["a_xT"], t3)
                transpose(b6, xn[(pi - 3) % 2], KD, "a_T")

        pe.wait_ge(s["small_in"], 16 * 8)
        pe.wait_ge(s["wa"], 2)
        pe.wait_ge(s["wv_s"], 2)
        pe.wait_ge(s["prep"], 4)
        skewed(pe, step_a, B, 7)

        def masked(bank, mask):
            pe.matmul(bank, ident_b[:], mask[:].unsqueeze(1).to_broadcast([P, 4, P]), start=True, stop=False,
                      skip_group_check=True)

        def scores(g, t, u):
            if g == 0:
                pe.wait_ge(s["h_qkT"], 6 * (t + 1))
            if due(4 * t + g):
                pe.wait_ge(s["h_max"], 4 * t + g)
            masked(b1, mask_qk)
            for j in range(4):
                blk, f = 4 * (g % 2) + j, g // 2
                ins = pe.matmul(b1[:, j * P:(j + 1) * P], qT[u][:, blk, :], kT[u][f][:, blk, :], start=False,
                                stop=True, skip_group_check=True)
            ins.then_inc(s["h_S1"], 1)

        def scores_again(g, t, u):
            if g == 0:
                pe.wait_ge(s["h_aug"], 64 * (t + 1))
            if due(4 * t + g):
                pe.wait_ge(s["h_exp"], 4 * t + g)
            masked(b2, mask_kq)
            for j in range(4):
                blk, f = 4 * (g % 2) + j, g // 2
                ins = pe.matmul(b2[:, j * P:(j + 1) * P], kT[u][f][:, blk, :], qT[u][:, blk, :], start=False,
                                stop=True, skip_group_check=True)
            ins.then_inc(s["h_S2"], 1)

        def times_values(g, t, u):
            if g == 0:
                pe.wait_ge(s["h_va"], t + 1)
                if due(t):
                    pe.wait_ge(s["h_o"], t)
            pe.wait_ge(s["h_exp"], 4 * t + g + 1)
            for j in range(4):
                slot = 4 * g + j
                hd = slot % NB * 2 + slot // NB
                ins = pe.matmul(b4[32 * j:32 * (j + 1), g * P:(g + 1) * P], vaug[u][:, hd, :], PT[:, slot, :],
                                start=True, stop=True)
            if g == 3:
                ins.then_inc(s["h_AV"], 1)

        def pad_T(r, t):
            if r == 0:
                pe.wait_ge(s["h_dup"], 2 * (t + 1))
                pe.wait_ge(s["h_lo"], 2 * (t + 1))
            read = 6 * t + (0, 1, 2, 4)[r]
            if due(read):
                pe.wait_ge(s["h_qkT"], read)
            for n in range(4):
                hd = 2 * (4 * (r % 2) + n)
                ins = pe.transpose(b0[:, n * P:(n + 1) * P],
                                   pad[:, r // 2, hd:hd + 2, :].rearrange("p a b -> p (a b)").bitcast(F32), ident[:])
            ins.then_inc(s["h_padT"], 1)

        def step_b(i, pi):
            t2, t3, t8, t9, t10 = (at(i, k) for k in (2, 3, 8, 9, 10))

            def experts(r):
                if due(E * t10 + 2 * r - 2):
                    pe.wait_ge(s["c_es"], E * t10 + 2 * r - 2)
                product(PS[:, r % 2, :], kt(eT[pi % 2]), kt(w_e, 2 * r * D, 2 * (r + 1) * D), "c_exp")

            def summed(r):
                if r == 0:
                    if due(t10):
                        pe.wait_ge(s["c_acc"], t10)
                    pe.matmul(b2[:, 0:D], ident[:], tile(x2, t10), start=True, stop=False)
                    pe.matmul(b2[:, 0:D], ident[:], tile(h, t10), start=False, stop=False)
                for e in (2 * r, 2 * r + 1):
                    pe.wait_ge(s["c_es"], E * t10 + e + 1)
                    ins = pe.matmul(b2[:, 0:D], ident[:], es[:, e, :], start=False, stop=e == E - 1)
                ins.then_inc(s["c_sum"], 1)

            if t8 is not None:
                pe.wait_ge(s["g_o"], t8 + 1)
                if due(t8):
                    pe.wait_ge(s["g_upd"], t8)
                transpose(b4[:, D:2 * D], o_sb, KD, "g_oT")
            if t3 is not None:
                u = (pi - 3) % 2
                pe.wait_ge(s["b_xT"], t3 + 1)
                if due(t3):
                    pe.wait_ge(s["b_qf"], t3)
                pe.matmul(b7[:, 0:D], ident[:], b_q, start=True, stop=False)
                for k in range(KD):
                    ins = pe.matmul(b7[:, 0:D], xT[u][:, k, :], w_q[:, k, :], start=False, stop=k == KD - 1)
                ins.then_inc(s["b_q"], 1)
                if due(done(i, 10)):
                    pe.wait_ge(s["c_lb"], done(i, 10))
                product(b5[0:LAT, 0:P], kt(w_down), kt(xT[u]), "b_c")
            if t10 is not None:
                pe.wait_ge(s["c_xT"], t10 + 1)
                experts(0)
                experts(1)
            if t8 is not None:
                pe.wait_ge(s["g_oTs"], t8 + 1)
                pe.matmul(b4[:, 0:D], ident[:], tile(x2, t8), start=True, stop=False)
                pe.matmul(b4[:, 0:D], ident[:], b_o, start=False, stop=False)
                for k in range(KD):
                    ins = pe.matmul(b4[:, 0:D], oT[:, k, :], w_o0[:, k, :], start=False, stop=k == KD - 1)
                ins.then_inc(s["g_Wo"], 1)
            if t3 is not None:
                pe.wait_ge(s["b_cT"], t3 + 1)
                if due(t3):
                    pe.wait_ge(s["b_vf"], t3)
                product(b3, [cT], [w_up], "b_kv")
            if t10 is not None:
                summed(0)
                experts(2)
                summed(1)
                experts(3)
            if t9 is not None:
                pe.wait_ge(s["c_xn"], t9 + 1)
                transpose(b6[:, D:2 * D], en[(pi - 9) % 2], KD, "c_T")
            if t10 is not None:
                summed(2)
            if t9 is not None:
                pe.wait_ge(s["c_xT"], t9 + 1)
                if due(done(i, 3)):
                    pe.wait_ge(s["b_cT"], done(i, 3))
                product(b5[:, P:P + E], kt(eT[(pi - 9) % 2]), kt(w_g), "c_lg")
            if t2 is not None:
                pe.wait_ge(s["b_xn"], t2 + 1)
                transpose(b6, xn[pi % 2], KD, "b_T")
            if t10 is not None:
                summed(3)

        pe.wait_ge(s["a_done"], B)
        pe.wait_ge(s["wf_s"], 8)
        skewed(pe, step_b, B, 11)

        def step_d(i, pi):
            t1_, t2, t4, t5, t6, t7, t9 = (at(i, k) for k in (1, 2, 4, 5, 6, 7, 9))
            u5 = (pi - 5) % 2
            if t7 is not None:
                pe.wait_ge(s["h_OTs"], t7 + 1)
                transpose(b4, ots, 4, "h_OTT")
            if t2 is not None:
                pe.wait_ge(s["d_xT"], t2 + 1)
                if due(3 * t2):
                    pe.wait_ge(s["d_rot"], 3 * t2)
                product(b3, kt(xT[pi % 2]), kt(w_qk1), "d_qk")
            if t1_ is not None:
                pe.wait_ge(s["d_xn"], t1_ + 1)
                if due(done(i, 8)):
                    pe.wait_ge(s["h_upd"], done(i, 8))
                transpose(b6, xn[(pi - 1) % 2], KD, "d_T")
            if t5 is not None:
                scores(0, t5, u5)
            if t9 is not None:
                pe.wait_ge(s["e_xn"], t9 + 1)
                if due(done(i, 1)):
                    pe.wait_ge(s["d_xT"], done(i, 1))
                transpose(b6[:, D:2 * D], en[(pi - 9) % 2], KD, "e_T")
            if t2 is not None:
                if due(t2):
                    pe.wait_ge(s["d_vf"], t2)
                if due(done(i, 8)):
                    pe.wait_ge(s["h_oTs"], done(i, 8))
                product(b7[:, 0:D], kt(xT[pi % 2]), kt(w_v1), "d_v")
            if t6 is not None:
                scores_again(0, t6, pi % 2)
            if t5 is not None:
                scores(1, t5, u5)
            if t6 is not None:
                scores_again(1, t6, pi % 2)
                times_values(0, t6, pi % 2)
            if t9 is not None:
                pe.wait_ge(s["e_xT"], t9 + 1)
                if due(done(i, 6)):
                    pe.wait_ge(s["h_nTs"], done(i, 6))
                product(b5[:, 0:E], kt(eT[0]), kt(w_router), "e_lg")
            if t6 is not None:
                scores_again(2, t6, pi % 2)
                times_values(1, t6, pi % 2)
            if t5 is not None:
                scores(2, t5, u5)
            if t4 is not None:
                pad_T(0, t4)
            if t7 is not None:
                pe.wait_ge(s["h_o"], t7 + 1)
                if due(done(i, 2)):
                    pe.wait_ge(s["d_vf"], done(i, 2))
                transpose(b7[:, D:2 * D], o_sb, KD, "h_oT")
            if t6 is not None:
                scores_again(3, t6, pi % 2)
                times_values(2, t6, pi % 2)
            if t5 is not None:
                scores(3, t5, u5)
            if t4 is not None:
                pad_T(1, t4)
            if t7 is not None:
                pe.wait_ge(s["h_oTs"], t7 + 1)
                if due(done(i, 9)):
                    pe.wait_ge(s["e_xT"], done(i, 9))
                if due(done(i, 1)):
                    pe.wait_ge(s["d_xT"], done(i, 1))
                product(b6[:, 0:D], kt(oT), kt(w_o1), "h_Wo")
            if t5 is not None:
                pe.wait_ge(s["h_nl"], t5 + 1)
                if due(done(i, 9)):
                    pe.wait_ge(s["e_lgs"], done(i, 9))
                pe.transpose(b5[:, P:2 * P], nms[:].bitcast(F32), ident[:]).then_inc(s["h_nT"], 1)
            if t4 is not None:
                pad_T(2, t4)
            if t6 is not None:
                times_values(3, t6, pi % 2)
            if t4 is not None:
                pad_T(3, t4)

        pe.wait_ge(s["c_acc"], B)
        pe.wait_ge(s["masks"], 6)
        pe.wait_ge(s["ident_b"], 1)
        pe.wait_ge(s["w1_in"], 16 * 7)
        skewed(pe, step_d, B, 10)

        pe.wait_ge(s["e_lgs"], B)
        pe.wait_ge(s["r_dve"], 6)
        hot = r_hot_b
        pe.matmul(b0[:, 0:B * E], before[:], hot.rearrange("p b e -> p (b e)"), start=True, stop=False,
                  skip_group_check=True)
        for d in range(1, B):
            pe.matmul(b0[:, d * E:B * E], ones_b[:], hot[:, 0:B - d, :].rearrange("p b e -> p (b e)"),
                      start=False, stop=d == B - 1, skip_group_check=True)
        for t in range(B):
            ins = pe.matmul(b1[:, 0:E], ones_b[:], hot[:, t, :], start=t == 0, stop=t == B - 1)
        ins.then_inc(s["r_pe"], 1)
        pe.wait_ge(s["r_hots"], 3)
        for t in range(B):
            for n in range(2):
                ins = pe.matmul(b2[:, 0:NJ], r_hot_c[:, t, :], r_token[n][:, t, :],
                                start=t == 0 and n == 0, stop=t == B - 1 and n == 1)
        ins.then_inc(s["r_pe"], 1)

        def gate_or_up(e, u, half, name):
            for n in range(2):
                for k in range(KD):
                    lo = (k * 2 + half) * I + n * IH
                    w = W[:, bass.ds(e, 1), lo:lo + IH].rearrange("p a d -> p (a d)")
                    ins = pe.matmul(PS[:, 1 + 2 * half + n, 0:IH], xsT[u][:, k, :], w, start=k == 0, stop=k == KD - 1)
            ins.then_inc(s[name], 1)

        def step_f(i, pi):
            j4, j3, j2, j1 = (at(i, k, NJ) for k in (4, 3, 2, 1))
            if j4 is not None:
                u = pi % 2
                e = pe.value_load(texp_i[0:1, bass.ds(j4, 1)], min_val=0, max_val=E - 1)
                pe.wait_ge(s["f_hTa"], j4 + 1)
                pe.wait_ge(s["f_hTb"], j4 + 1)
                if due(j4):
                    pe.wait_ge(s["f_y"], j4)
                for k in range(KI):
                    r = P if k < KI - 1 else IR
                    w = W[0:r, bass.ds(e, 1), GU + k * D:GU + (k + 1) * D].rearrange("p a d -> p (a d)")
                    ins = pe.matmul(b7[:, 0:D], hT[u][0:r, k, :], w, start=k == 0, stop=k == KI - 1)
                ins.then_inc(s["f_down"], 1)
            if j2 is not None:
                u = pi % 2
                e = pe.value_load(texp_i[0:1, bass.ds(j2, 1)], min_val=0, max_val=E - 1)
                pe.wait_ge(s["f_xT"], j2 + 1)
                if due(j2):
                    pe.wait_ge(s["f_silu"], j2)
                gate_or_up(e, u, 0, "f_gate")
            if j3 is not None:
                uh = (pi - 3) % 2
                pe.wait_ge(s["f_hm"], j3 + 1)
                for bank, name, done in ((b5, "f_Ta", "f_hTa"), (b6, "f_Tb", "f_hTb")):
                    if due(j3):
                        pe.wait_ge(s[done], j3)
                    for n in range(3):
                        k = n if bank is b5 else n + 3
                        w = P if k < KI - 1 else IR
                        ins = pe.transpose(bank[0:w, n * P:(n + 1) * P], hm[uh][:, k * P:k * P + w], ident[:])
                    ins.then_inc(s[name], 1)
            if j2 is not None:
                if due(j2):
                    pe.wait_ge(s["f_hm"], j2)
                gate_or_up(e, u, 1, "f_up")
            if j1 is not None:
                u = (pi - 1) % 2
                pe.wait_ge(s[f"f_xin{u}"], 8 * (j1 - u) + 16)
                if due(j1):
                    pe.wait_ge(s["f_xT"], j1)
                transpose(b0, gx[u], KD, "f_T")

        pe.wait_ge(s["experts_in"], 16 * 4 * E)
        pe.wait_ge(s["r_tables"], 1)
        skewed(pe, step_f, NJ, 5)

    @block.scalar
    def _(act):
        def copy(dst, src, sem, **k):
            act.activation(dst, src, ACT.Copy, **k).then_inc(s[sem], 1)

        for k in range(KD):
            act.wait_ge(s["wv_mx"], k + 1)
            act.activation(w_vs[:, k, :], w_vs[:, k, :], ACT.Exp, bias=wv_small[:, k:k + 1],
                           accum_out=wv_small[:, 2 + k:3 + k]).then_inc(s["wv_ex"], 1)
        for c in range(KD):
            act.wait_ge(s["wa_ps"], c + 1)
            copy(w_a[:, c, :], PS[:, c, 0:D], "wa")

        def step_a(i, pi):
            t3, t4, t5, t6 = (at(i, k) for k in (3, 4, 5, 6))
            if t6 is not None:
                count = ready(act, t6 + 1)
                act.wait_ge(s["w0_in"], 48)
                act.wait_ge(s["a_O"], count)
                copy(tile(h, t6), b4[:, 0:D], "a_done")
            if t5 is not None:
                u = (pi - 5) % 2
                act.wait_ge(s["a_mx"], t5 + 1)
                if due(t5 - 1):
                    act.wait_ge(s["a_O"], t5 - 1)
                act.activation(ET[u], b1[:, 0:P], ACT.Exp, bias=sm[u][:, 0:1], scale=SCALE0,
                               accum_out=sm[u][:, 1:2]).then_inc(s["a_E"], 1)
            if t4 is not None:
                u = pi % 2
                act.wait_ge(s["a_u"], t4 + 1)
                if due(t4 - 1):
                    act.wait_ge(s["a_S"], t4 - 1)
                copy(uT[u].rearrange("p k t -> p (k t)"), b3[:, 0:D], "a_uT")
                act.wait_ge(s["a_v"], t4 + 1)
                if due(t4 - 1):
                    act.wait_ge(s["a_O"], t4 - 1)
                copy(va_[u], b7[:, 0:D], "a_vs")
            if t3 is not None:
                act.wait_ge(s["a_T"], t3 + 1)
                if due(t3 - 1):
                    act.wait_ge(s["a_S"], t3 - 1)
                copy(xT[(pi - 3) % 2].rearrange("p k t -> p (k t)"), b6[:, 0:D], "a_xT")
            if t5 is not None:
                u = (pi - 5) % 2
                act.wait_ge(s["a_ri"], t5 + 1)
                act.wait_ge(s["a_vs"], t5 + 1)
                if due(t5):
                    act.wait_ge(s["a_O"], t5)
                copy(vn, va_[u], "a_vn", scale=sm[u][:, 2:3])

        act.wait_ge(s["w0_in"], 48)
        skewed(act, step_a, B, 7)

        act.wait_ge(s["wf_in"], 16 * 20)
        for k in range(KD):
            for w in (w_q, w_down):
                copy(w[:, k, :], w[:, k, :], "wf_s", scale=col[:, k:k + 1])
            for w in (w_e, w_g):
                copy(w[:, k, :], w[:, k, :], "wf_s", scale=col[:, 2 + k:3 + k])

        def high(t, u, name):
            act.wait_ge(s[name], t + 1)
            if due(4 * t):
                act.wait_ge(s["h_padT"], 4 * t)
            copy(pad[:, :, :, 0:HD], qkf[u], "h_hi")

        def step_b(i, pi):
            t1_, t2, t3, t5, t8, t9, t10 = (at(i, k) for k in (1, 2, 3, 5, 8, 9, 10))

            def by_gates(r):
                u = pi % 2
                if r == 0:
                    act.wait_ge(s["c_gt"], t10 + 1)
                act.wait_ge(s["c_exp"], 4 * t10 + r + 1)
                if due(4 * t10):
                    act.wait_ge(s["c_sum"], 4 * t10)
                for e in (2 * r, 2 * r + 1):
                    lo = e % 2 * D
                    copy(es[:, e, :], PS[:, r % 2, lo:lo + D], "c_es", scale=gate[u][:, e:e + 1])

            def squares(x, src, t, made):
                n, base = NORMS[x]
                free, before_, count = ready(act, base + t - 1), ready(act, base + t), ready(act, t + 1)
                act.wait_ge(s["wf_s"], 8)
                act.wait_ge(s[made], count)
                if due(free):
                    act.wait_ge(s[f"n{n}_rs"], free)
                if due(before_):
                    act.wait_ge(s[f"n{n}_ag"], before_)
                act.activation(ots[:, (n - 1) * D:n * D], src, ACT.Square, accum_out=mv[n][(pi - (n == 1)) % 2][:, 0:1]
                               ).then_inc(s[f"n{n}_ag"], 1)

            if t8 is not None:
                act.wait_ge(s["g_oT"], t8 + 1)
                if due(t8):
                    act.wait_ge(s["g_Wo"], t8)
                copy(oT.rearrange("p k t -> p (k t)"), b4[:, D:2 * D], "g_oTs")
            if t3 is not None:
                act.wait_ge(s["b_q"], t3 + 1)
                if due(4 * (t3 - 1)):
                    act.wait_ge(s["g_qk_mul"], 4 * (t3 - 1))
                copy(qkf[(pi - 3) % 2][:, 0].rearrange("p h d -> p (h d)"), b7[:, 0:D], "b_qf")
                act.wait_ge(s["b_c"], t3 + 1)
                if due(t3):
                    act.wait_ge(s["b_kv"], t3)
                act.activation(cT, b5[0:LAT, 0:P], ACT.Identity, bias=col[0:LAT, 4:5]).then_inc(s["b_cT"], 1)
            if t10 is not None:
                by_gates(0)
                by_gates(1)
            if t8 is not None:
                count = ready(act, t8 + 1)
                act.wait_ge(s["wf_s"], 8)
                act.wait_ge(s["g_Wo"], count)
                copy(tile(x2, t8), b4[:, 0:D], "g_upd")
                squares("c0", tile(x2, t8), t8, "g_upd")
            if t10 is not None:
                by_gates(2)
                by_gates(3)
            if t9 is not None:
                act.wait_ge(s["c_T"], t9 + 1)
                if due(4 * (t9 - 1)):
                    act.wait_ge(s["c_exp"], 4 * (t9 - 1))
                copy(eT[(pi - 9) % 2].rearrange("p k t -> p (k t)"), b6[:, D:2 * D], "c_xT")
            if t5 is not None:
                u = (pi - 5) % 2
                act.wait_ge(s["g_sub"], t5 + 1)
                act.activation(sc[u], sc[u], ACT.Exp, scale=SCALEH).then_inc(s["g_exp"], 1)
            if t2 is not None:
                act.wait_ge(s["b_T"], t2 + 1)
                if due(t2 - 1):
                    act.wait_ge(s["b_q"], t2 - 1)
                    act.wait_ge(s["b_c"], t2 - 1)
                copy(xT[pi % 2].rearrange("p k t -> p (k t)"), b6[:, 0:D], "b_xT")
            if t10 is not None:
                count = ready(act, 4 * t10 + 4)
                act.wait_ge(s["wf_s"], 8)
                act.wait_ge(s["c_sum"], count)
                copy(tile(h, t10), b2[:, 0:D], "c_acc")
            if t9 is not None:
                u = (pi - 9) % 2
                act.wait_ge(s["c_mx"], t9 + 1)
                if due(t9 - 1):
                    act.wait_ge(s["c_gt"], t9 - 1)
                act.activation(gate[u], glog, ACT.Exp, bias=gmax[:, 0:1], accum_out=gsum[u][:, 0:1]
                               ).then_inc(s["c_ex"], 1)
            if t1_ is not None:
                squares("b1", tile(x2, t1_), t1_, "b_x2")

        act.wait_ge(s["a_done"], B)
        act.wait_ge(s["wf_s"], 8)
        skewed(act, step_b, B, 11)

        def step_d(i, pi):
            t1_, t2, t3, t4, t5, t6, t7, t9 = (at(i, k) for k in (1, 2, 3, 4, 5, 6, 7, 9))

            def exponentials(g):
                act.wait_ge(s["h_S2"], 4 * t6 + g + 1)
                if due(t6):
                    act.wait_ge(s["h_AV"], t6)
                act.activation(PT[:, 4 * g:4 * g + 4, :].rearrange("p h t -> p (h t)"), b2, ACT.Exp,
                               scale=SCALEH).then_inc(s["h_exp"], 1)

            if t1_ is not None:
                act.wait_ge(s["d_T"], t1_ + 1)
                if due(t1_ - 1):
                    act.wait_ge(s["d_v"], t1_ - 1)
                copy(xT[(pi - 1) % 2].rearrange("p k t -> p (k t)"), b6[:, 0:D], "d_xT")
            if t9 is not None:
                act.wait_ge(s["e_T"], t9 + 1)
                if due(t9):
                    act.wait_ge(s["e_lg"], t9)
                copy(eT[0].rearrange("p k t -> p (k t)"), b6[:, D:2 * D], "e_xT")
            if t2 is not None:
                act.wait_ge(s["d_v"], t2 + 1)
                copy(tile(v_tiles, t2), b7[:, 0:D], "d_vf")
            if t6 is not None:
                exponentials(0)
            if t6 is not None:
                exponentials(1)
            if t9 is not None:
                act.wait_ge(s["e_lg"], t9 + 1)
                copy(tile(LG, t9), b5[:, 0:E], "e_lgs")
            if t6 is not None:
                exponentials(2)
            if t4 is not None:
                qk_out(act, t4, pi % 2, 0)
            if t7 is not None:
                act.wait_ge(s["h_oT"], t7 + 1)
                if due(t7):
                    act.wait_ge(s["h_Wo"], t7)
                copy(oT.rearrange("p k t -> p (k t)"), b7[:, D:2 * D], "h_oTs")
            if t6 is not None:
                exponentials(3)
            if t5 is not None:
                act.wait_ge(s["h_nT"], t5 + 1)
                if due(64 * t5):
                    act.wait_ge(s["h_aug"], 64 * t5)
                copy(nmT[:], b5[0:32, P:2 * P], "h_nTs")
            if t4 is not None:
                qk_out(act, t4, pi % 2, 2, 0)
            if t6 is not None:
                act.wait_ge(s["h_AV"], t6 + 1)
                if due(t6):
                    act.wait_ge(s["h_OTT"], t6)
                copy(ots, b4, "h_OTs")
            if t4 is not None:
                qk_out(act, t4, pi % 2, 3, 0)
            if t3 is not None:
                high(t3, (pi - 3) % 2, "d_qf")

        act.wait_ge(s["c_acc"], B)
        act.wait_ge(s["masks"], 6)
        skewed(act, step_d, B, 10)

        def step_f(i, pi):
            j = at(i, 3, NJ)
            if j is not None:
                act.wait_ge(s["f_Ta"], j + 1)
                if due(j - 1):
                    act.wait_ge(s["f_down"], j - 1)
                copy(hT[(pi - 3) % 2][:, 0:3, :].rearrange("p k t -> p (k t)"), b5[:, 0:3 * P], "f_hTa")
            j = at(i, 2, NJ)
            if j is not None:
                act.wait_ge(s["f_gate"], j + 1)
                if due(j):
                    act.wait_ge(s["f_hm"], j)
                act.activation(sg.rearrange("p (n i) -> p n i", n=2), PS[:, 1:3, 0:IH], ACT.Silu
                               ).then_inc(s["f_silu"], 1)

        act.wait_ge(s["r_pe"], 1)
        act.activation(neghalf[:], neghalf[:], ACT.Silu).then_inc(s["f_warm"], 1)
        act.wait_ge(s["f_warm"], 1)
        act.wait_ge(s["r_tables"], 1)
        skewed(act, step_f, NJ, 5)

    @block.vector
    def _(dve):
        def stats(x, src, u, t):
            n = NORMS[x][0]
            dve.bn_stats(stat[n][:], src).then_inc(s[f"n{n}_st"], 1)
            count = ready(dve, TAKEN[x] + t + 1)
            dve.wait_ge(s["small_in"], 16 * 8)
            dve.wait_ge(s[f"n{n}_st"], count)
            dve.bn_aggr(mv[n][u][:], stat[n][:]).then_inc(s[f"n{n}_ag"], 1)

        def rs_ready(x, t):
            n, base = NORMS[x]
            dve.wait_ge(s[f"n{n}_rs"], base + t + 1)

        def normed(dst, src, n, u, sem):
            dve.tensor_scalar(dst, src, mv[n][u][:, 0:1], rs[n][u][:, 1:2], ALU.subtract, ALU.mult
                              ).then_inc(s[sem], 1)

        dve.wait_ge(s["w0_in"], 48)
        for k in range(KD):
            dve.tensor_reduce(wv_small[:, k:k + 1], w_vs[:, k, :], AX.X, ALU.max, negate=True).then_inc(s["wv_mx"], 1)
        for k in range(KD):
            dve.wait_ge(s["wv_ex"], k + 1)
            dve.reciprocal(wv_small[:, 4 + k:5 + k], wv_small[:, 2 + k:3 + k]).then_inc(s["wv_ri"], 1)
            dve.wait_ge(s["wv_ri"], k + 1)
            dve.tensor_scalar(w_vs[:, k, :], w_vs[:, k, :], wv_small[:, 4 + k:5 + k], 1.0 / D, ALU.mult, ALU.mult
                              ).then_inc(s["wv_s"], 1)
        dve.wait_ge(s["small_in"], 16 * 8)
        dve.tensor_copy(ident_b[:], ident[:]).then_inc(s["ident_b"], 1)
        dve.tensor_copy(typ, typ_i[:]).then_inc(s["prep"], 1)
        dve.tensor_tensor(pos_t, pos_t, t01[:, 0, :], ALU.add).then_inc(s["prep"], 1)
        dve.tensor_tensor(dtype_, t01[:, 1, :], t01[:, 0, :], ALU.subtract).then_inc(s["prep"], 1)
        dve.tensor_scalar(minus_ident, ident[:], -1.0, None, ALU.mult).then_inc(s["prep"], 1)
        dve.wait_ge(s["prep"], 4)

        def step_a(i, pi):
            t1_, t2, t3, t5 = (at(i, k) for k in (1, 2, 3, 5))
            if t3 is not None:
                rs_ready("a1", t3)
                if due(t3 - 1):
                    dve.wait_ge(s["a_T"], t3 - 1)
                normed(xn[(pi - 3) % 2], tile(h, t3), 1, (pi - 3) % 2, "a_xn")
            if t5 is not None:
                u = (pi - 5) % 2
                dve.wait_ge(s["a_S"], t5 + 1)
                dve.tensor_reduce(sm[u][:, 3:4], b1[:, 0:P], AX.X, ALU.max, negate=True).then_inc(s["a_mr"], 1)
                dve.wait_ge(s["a_mr"], t5 + 1)
                if due(t5 - 1):
                    dve.wait_ge(s["a_E"], t5 - 1)
                dve.tensor_scalar(sm[u][:, 0:1], sm[u][:, 3:4], SCALE0, None, ALU.mult).then_inc(s["a_mx"], 1)
            if t1_ is not None:
                u = (pi - 1) % 2
                dve.wait_ge(s["a_x"], t1_ + 1)
                dve.scalar_tensor_tensor(tile(h, t1_), dtype_, typ[:, bass.ds(t1_, 1)], tile(h, t1_), ALU.mult,
                                         ALU.add).then_inc(s["a_xt"], 1)
                count = ready(dve, t1_ + 1)
                dve.wait_ge(s["small_in"], 16 * 8)
                dve.wait_ge(s["a_xt"], count)
                stats("a0", tile(h, t1_), u, t1_)
            if t5 is not None:
                u = (pi - 5) % 2
                dve.wait_ge(s["a_E"], t5 + 1)
                dve.reciprocal(sm[u][:, 2:3], sm[u][:, 1:2]).then_inc(s["a_ri"], 1)
            if t2 is not None:
                u = pi % 2
                rs_ready("a0", t2)
                dve.scalar_tensor_tensor(n0, tile(h, t2), mv[0][u][:, 0:1], gam, ALU.subtract, ALU.mult
                                         ).then_inc(s["a_ng"], 1)
                dve.wait_ge(s["a_ng"], t2 + 1)
                dve.scalar_tensor_tensor(tile(h, t2), n0, rs[0][u][:, 1:2], bet, ALU.mult, ALU.add
                                         ).then_inc(s["a_h"], 1)
                count = ready(dve, t2 + 1)
                dve.wait_ge(s["small_in"], 16 * 8)
                dve.wait_ge(s["a_h"], count)
                stats("a1", tile(h, t2), u, t2)

        skewed(dve, step_a, B, 7)
        dve.wait_ge(s["a_done"], B)

        def normalise(i):
            t = at(i, 7)
            if t is not None:
                dve.wait_ge(s["h_OTT"], t + 1)
                heads_ = b4.rearrange("p (h c) -> p h c", h=H)
                dve.reciprocal(rinv[:].unsqueeze(2), heads_[:, :, HD:HD + 1]).then_inc(s["h_ri"], 1)
                dve.wait_ge(s["h_ri"], t + 1)
                if due(t):
                    dve.wait_ge(s["h_oT"], t)
                dve.tensor_tensor(o_sb.rearrange("p (b f d) -> p f b d", f=2, d=HD),
                                  heads_[:, :, 0:HD].rearrange("p (f b) d -> p f b d", f=2),
                                  rinv[:].rearrange("p (f b) -> p f b", f=2).unsqueeze(3).to_broadcast([P, 2, NB, HD]),
                                  ALU.mult).then_inc(s["h_o"], 1)

        def maxima(g, t):
            dve.wait_ge(s["h_S1"], 4 * t + g + 1)
            dve.tensor_reduce(nmax[:, 4 * g:4 * g + 4], b1.rearrange("p (h k) -> p h k", h=4), AX.X, ALU.max,
                              negate=True).then_inc(s["h_max"], 1)

        def split_maxima(t):
            split = nms[:, 0:32].rearrange("p (f a b) -> p f a b", f=2, a=2)
            whole = nmax[:].rearrange("p (f b) -> p f b", f=2)
            dve.wait_ge(s["h_max"], 4 * t + 4)
            if due(t):
                dve.wait_ge(s["h_nT"], t)
            dve.tensor_copy(split[:, :, 0, :], whole).then_inc(s["h_nh"], 1)
            dve.wait_ge(s["h_nh"], t + 1)
            dve.tensor_tensor(split[:, :, 1, :], whole, split[:, :, 0, :].bitcast(F32), ALU.subtract
                              ).then_inc(s["h_nl"], 1)

        def low(t, u):
            dve.wait_ge(s["h_hi"], t + 1)
            for x, at_ in ((0, HD), (1, 2 * HD)):
                dve.tensor_tensor(pad[:, x, :, at_:at_ + HD], qkf[u][:, x], pad[:, x, :, 0:HD].bitcast(F32),
                                  ALU.subtract).then_inc(s["h_lo"], 1)

        def step_b(i, pi):
            t1_, t2, t3, t5, t6, t7, t8, t9, t10 = (at(i, k) for k in (1, 2, 3, 5, 6, 7, 8, 9, 10))
            t0 = at(i, 0)
            if t10 is not None:
                u = pi % 2
                dve.wait_ge(s["c_ex"], t10 + 1)
                dve.reciprocal(gsum[u][:, 1:2], gsum[u][:, 0:1]).then_inc(s["c_ri"], 1)
                dve.wait_ge(s["c_ri"], t10 + 1)
                dve.tensor_scalar(gate[u], gate[u], gsum[u][:, 1:2], None, ALU.mult).then_inc(s["c_gt"], 1)
            if t7 is not None:
                u = (pi - 7) % 2
                for lo, hi, name in ((0, HP, "g_pv_pool"), (HP, H, "g_pv_dve")):
                    dve.wait_ge(s[name], t7 + 1)
                    if lo == 0:
                        if due(t7):
                            dve.wait_ge(s["g_oT"], t7)
                    dve.tensor_reduce(o_heads[:, lo:hi], heads3(pv)[:, lo:hi], AX.X, ALU.add).then_inc(s["g_O"], 1)
                dve.wait_ge(s["g_ri"], t7 + 1)
                dve.wait_ge(s["g_O"], 2 * t7 + 2)
                dve.tensor_tensor(o_heads, o_heads, rsum[u].unsqueeze(2).to_broadcast([P, H, HD]), ALU.mult
                                  ).then_inc(s["g_o"], 1)
            if t9 is not None:
                rs_ready("c0", t9)
                if due(t9 - 1):
                    dve.wait_ge(s["c_T"], t9 - 1)
                dve.tensor_scalar(en[(pi - 9) % 2], tile(x2, t9), rs[2][(pi - 9) % 2][:, 1:2], None, ALU.mult
                                  ).then_inc(s["c_xn"], 1)
            if t2 is not None:
                rs_ready("b1", t2)
                if due(t2 - 1):
                    dve.wait_ge(s["b_T"], t2 - 1)
                dve.tensor_scalar(xn[pi % 2], tile(x2, t2), rs[1][pi % 2][:, 1:2], None, ALU.mult
                                  ).then_inc(s["b_xn"], 1)
            if t1_ is not None:
                rs_ready("b0", t1_)
                normed(tile(x2, t1_), tile(h, t1_), 0, (pi - 1) % 2, "b_x2")
            if t5 is not None:
                u = (pi - 5) % 2
                for g in range(4):
                    dve.wait_ge(s["g_qk_mul"], 4 * t5 + g + 1)
                    if g == 0:
                        if due(t5 - 1):
                            dve.wait_ge(s["g_pv_pool"], t5 - 1)
                            dve.wait_ge(s["g_pv_dve"], t5 - 1)
                            dve.wait_ge(s["g_sum"], t5 - 1)
                    dve.tensor_reduce(sc[u][:, 4 * g:4 * g + 4], heads3(qk)[:, 4 * g:4 * g + 4], AX.X, ALU.add
                                      ).then_inc(s["g_S"], 1)
            if t5 is not None:
                dve.wait_ge(s["g_S"], 4 * t5 + 4)
                dve.tensor_reduce(hmax, sc[u], AX.X, ALU.max).then_inc(s["g_max"], 1)
                dve.wait_ge(s["g_max"], t5 + 1)
                dve.tensor_tensor(sc[u], sc[u], hmax.unsqueeze(2).to_broadcast([P, H, H]), ALU.subtract
                                  ).then_inc(s["g_sub"], 1)
            if t6 is not None:
                u = pi % 2
                dve.wait_ge(s["g_exp"], t6 + 1)
                if due(t6 - 1):
                    dve.wait_ge(s["g_o"], t6 - 1)
                dve.tensor_reduce(rsum[u], sc[u], AX.X, ALU.add).then_inc(s["g_sum"], 1)
                dve.wait_ge(s["g_sum"], t6 + 1)
                dve.reciprocal(rsum[u], rsum[u]).then_inc(s["g_ri"], 1)
                if due(2 * t6):
                    dve.wait_ge(s["g_O"], 2 * t6)
                dve.tensor_tensor(heads3(pv)[:, HP:H], over_keys(sc[u][:, HP:H]),
                                  over_queries(tile(v_tiles, t6), H - HP), ALU.mult).then_inc(s["g_pv_dve"], 1)
            if t3 is not None:
                u = (pi - 3) % 2
                kv = b3.rearrange("p (h c) -> p h c", h=H)
                bias = b_up.rearrange("p (h c) -> p h c", h=H)
                dve.wait_ge(s["b_kv"], t3 + 1)
                if due(4 * (t3 - 1)):
                    dve.wait_ge(s["g_qk_mul"], 4 * (t3 - 1))
                dve.tensor_tensor(qkf[u][:, 1], kv[:, :, 0:HD], bias[:, :, 0:HD], ALU.add).then_inc(s["b_kf"], 1)
                dve.tensor_tensor(over_heads(tile(v_tiles, t3)), kv[:, :, HD:2 * HD], bias[:, :, HD:2 * HD], ALU.add
                                  ).then_inc(s["b_vf"], 1)
            if t9 is not None:
                dve.wait_ge(s["c_lg"], t9 + 1)
                if due(t9):
                    dve.wait_ge(s["c_ex"], t9)
                dve.tensor_tensor(glog, b5[:, P:P + E], b_g, ALU.add).then_inc(s["c_lb"], 1)
                dve.wait_ge(s["c_lb"], t9 + 1)
                dve.tensor_reduce(gmax[:, 0:1], glog, AX.X, ALU.max, negate=True).then_inc(s["c_mx"], 1)
            if t0 is not None:
                stats("b0", tile(h, t0), pi, t0)

        skewed(dve, step_b, B, 11)

        def step_d(i, pi):
            t0, t1_, t2, t4, t5, t7, t8, t9 = (at(i, k) for k in (0, 1, 2, 4, 5, 7, 8, 9))
            if t1_ is not None:
                rs_ready("d0", t1_)
                if due(t1_ - 1):
                    dve.wait_ge(s["d_T"], t1_ - 1)
                normed(xn[(pi - 1) % 2], tile(h, t1_), 0, (pi - 1) % 2, "d_xn")
            normalise(i)
            if t4 is not None:
                low(t4, pi % 2)
            if t9 is not None:
                u = (pi - 9) % 2
                rs_ready("e1", t9)
                if due(t9 - 1):
                    dve.wait_ge(s["e_T"], t9 - 1)
                if due(8 * (t9 - u)):
                    dve.wait_ge(s[f"e_xout{u}"], 8 * (t9 - u))
                normed(en[u], tile(h, t9), 1, u, "e_xn")
            if t2 is not None:
                dve.wait_ge(s["d_qk"], t2 + 1)
                if due(t2):
                    dve.wait_ge(s["d_qf"], t2)
                qk = b3.rearrange("p (h d) -> p h d", d=HD)
                half = HD // 2
                dve.tensor_tensor(rot_a, qk, cosb.unsqueeze(1).to_broadcast([P, 2 * H, HD]), ALU.mult
                                  ).then_inc(s["d_rot"], 1)
                for lo, fro in ((0, half), (half, 0)):
                    dve.tensor_tensor(rot_b[:, :, lo:lo + half], qk[:, :, fro:fro + half],
                                      sinb[:, lo:lo + half].unsqueeze(1).to_broadcast([P, 2 * H, half]), ALU.mult
                                      ).then_inc(s["d_rot"], 1)
            if t5 is not None:
                maxima(0, t5)
            if t0 is not None:
                stats("d0", tile(h, t0), pi, t0)
            if t5 is not None:
                maxima(1, t5)
            if t8 is not None:
                count = ready(dve, t8 + 1)
                dve.wait_ge(s["small_in"], 16 * 8)
                dve.wait_ge(s["h_upd"], count)
                stats("e1", tile(h, t8), pi % 2, t8)
            if t5 is not None:
                maxima(2, t5)
                maxima(3, t5)
                split_maxima(t5)
            if t4 is not None:
                qk_out(dve, t4, pi % 2, 1)
                qk_out(dve, t4, pi % 2, 2, 1)
            if t7 is not None:
                dve.wait_ge(s["h_Wo"], t7 + 1)
                dve.tensor_tensor(tile(h, t7), b6[:, 0:D], tile(h, t7), ALU.add).then_inc(s["h_upd"], 1)
            if t4 is not None:
                qk_out(dve, t4, pi % 2, 3, 1)

        skewed(dve, step_d, B, 10)

        done = [0]

        def chain(ins):
            done[0] += 1
            ins.then_inc(s["r_dve"], 1)
            dve.wait_ge(s["r_dve"], done[0])

        def c_(name):
            lo, n = CST[name]
            return cst[:, lo:lo + n]

        dve.wait_ge(s["e_lgs"], B)
        chain(dve.tensor_reduce(r_max, LG[:], AX.X, ALU.max))
        chain(dve.tensor_tensor(r_tmp, LG[:], r_max.unsqueeze(2).to_broadcast([P, B, E]), ALU.is_ge))
        chain(dve.tensor_tensor(r_tmp, r_tmp, c_("rank").unsqueeze(1).to_broadcast([P, B, E]), ALU.mult))
        chain(dve.tensor_reduce(r_max, r_tmp, AX.X, ALU.max))
        chain(dve.tensor_tensor(r_hot, r_tmp, r_max.unsqueeze(2).to_broadcast([P, B, E]), ALU.is_equal))
        chain(dve.tensor_copy(r_hot_b, r_hot))
        dve.wait_ge(s["r_pe"], 1)
        chain(dve.tensor_tensor(r_cmp, b1[:, 0:E].unsqueeze(2).to_broadcast([P, E, B]),
                                c_("tiles").unsqueeze(1).to_broadcast([P, E, B]), ALU.is_gt))
        chain(dve.tensor_reduce(r_n, r_cmp, AX.X, ALU.add))
        chain(dve.tensor_copy(r_ci, r_n))
        for e in range(1, E):
            chain(dve.tensor_tensor(r_ci[:, e:e + 1], r_ci[:, e - 1:e], r_n[:, e:e + 1], ALU.add))
        chain(dve.tensor_tensor(r_base, r_ci, r_n, ALU.subtract))
        chain(dve.tensor_scalar(r_base, r_base, float(P), None, ALU.mult))
        chain(dve.tensor_tensor(r_tmp, b0[:, 0:B * E].rearrange("p (b e) -> p b e", b=B),
                                r_base.unsqueeze(1).to_broadcast([P, B, E]), ALU.add))
        chain(dve.tensor_tensor(r_tmp, r_tmp, r_hot, ALU.mult))
        chain(dve.tensor_reduce(r_slot, r_tmp, AX.X, ALU.add))
        chain(dve.tensor_copy(r_slot_i, r_slot))
        chain(dve.tensor_scalar(r_a_i, r_slot_i, 7, None, ALU.logical_shift_right))
        chain(dve.tensor_scalar(r_b_i, r_slot_i, P - 1, None, ALU.bitwise_and))
        chain(dve.tensor_copy(r_a, r_a_i))
        chain(dve.tensor_copy(r_b, r_b_i))
        chain(dve.tensor_tensor(r_hot_a, r_a.unsqueeze(2).to_broadcast([P, B, NJ]),
                                c_("slot_tile").unsqueeze(1).to_broadcast([P, B, NJ]), ALU.is_equal))
        dve.tensor_tensor(r_token[0], r_hot_a, c_("tiles").unsqueeze(2).to_broadcast([P, B, NJ]), ALU.mult
                          ).then_inc(s["r_hots"], 1)
        dve.tensor_scalar(r_token[1], r_hot_a, c_("number"), None, ALU.mult).then_inc(s["r_hots"], 1)
        dve.tensor_tensor(r_hot_c, r_b.unsqueeze(2).to_broadcast([P, B, P]),
                          c_("place").unsqueeze(1).to_broadcast([P, B, P]), ALU.is_equal).then_inc(s["r_hots"], 1)
        chain(dve.tensor_tensor(r_te, c_("slot_tile").unsqueeze(2).to_broadcast([P, NJ, E]),
                                r_ci.unsqueeze(1).to_broadcast([P, NJ, E]), ALU.is_ge))
        chain(dve.tensor_reduce(r_tile, r_te, AX.X, ALU.add))
        chain(dve.tensor_scalar(texp_i[:], r_tile, float(E - 1), None, ALU.min))
        dve.wait_ge(s["r_pe"], 2)
        chain(dve.tensor_copy(r_id, b2[:, 0:NJ]))
        chain(dve.tensor_scalar(r_far, r_id, 0.0, FAR, ALU.is_equal, ALU.mult))
        chain(dve.tensor_scalar(r_idg, r_id, -1.0, 0.0, ALU.add, ALU.max))
        chain(dve.tensor_copy(idx_i[:, 0, :], r_idg))
        chain(dve.tensor_tensor(idx_i[:, 1, :], r_idg, r_far, ALU.add))
        dve.sem_inc(s["r_tables"], 1)

        def step_f(i, pi):
            j = at(i, 4, NJ)
            if j is not None:
                u = pi % 2
                dve.wait_ge(s["f_down"], j + 1)
                dve.wait_ge(s[f"f_hin{u}"], 8 * (j - u) + 16)
                if due(8 * (j - u)):
                    dve.wait_ge(s[f"f_out{u}"], 8 * (j - u))
                dve.tensor_tensor(yo[u], b7[:, 0:D], gh[u], ALU.add).then_inc(s["f_y"], 1)
            j = at(i, 3, NJ)
            if j is not None:
                u = (pi - 3) % 2
                dve.wait_ge(s["f_Tb"], j + 1)
                if due(j - 1):
                    dve.wait_ge(s["f_down"], j - 1)
                dve.tensor_copy(hT[u][:, 3:5, :].rearrange("p k t -> p (k t)"), b6[:, 0:2 * P])
                dve.tensor_copy(hT[u][0:IR, 5, :], b6[0:IR, 2 * P:3 * P]).then_inc(s["f_hTb"], 1)
            j = at(i, 2, NJ)
            if j is not None:
                u = pi % 2
                dve.wait_ge(s["f_up"], j + 1)
                dve.wait_ge(s["f_silu"], j + 1)
                if due(j - 1):
                    dve.wait_ge(s["f_Tb"], j - 1)
                dve.tensor_tensor(hm[u].rearrange("p (n i) -> p n i", n=2), PS[:, 3:5, 0:IH],
                                  sg.rearrange("p (n i) -> p n i", n=2), ALU.mult).then_inc(s["f_hm"], 1)
            j = at(i, 1, NJ)
            if j is not None:
                u = (pi - 1) % 2
                dve.wait_ge(s["f_T"], j + 1)
                if due(j - 1):
                    dve.wait_ge(s["f_up"], j - 1)
                dve.tensor_copy(xsT[u].rearrange("p k t -> p (k t)"), b0[:, 0:D]).then_inc(s["f_xT"], 1)

        skewed(dve, step_f, NJ, 5)


CST = {"rank": (0, E), "tiles": (E, B), "slot_tile": (E + B, NJ), "number": (E + B + NJ, 1),
       "place": (E + B + NJ + 1, P)}


def constants():
    wide = E + B + NJ + 1 + P
    c = np.zeros((P, wide), np.float32)

    def put(name, v):
        lo, n = CST[name]
        c[:, lo:lo + n] = v

    put("rank", E - np.arange(E))
    put("tiles", P * np.arange(B))
    put("slot_tile", np.arange(NJ))
    put("number", np.arange(P)[:, None] + 1)
    put("place", np.arange(P))
    inv = (1.0 / 10000.0 ** (np.arange(0, HD, 2, dtype=np.float32) / HD)).astype(np.float32)
    f = np.outer(np.arange(P, dtype=np.float32), inv).astype(np.float32)
    cos = np.concatenate([np.cos(f), np.cos(f)], 1).astype(np.float32)
    sin = np.concatenate([-np.sin(f), np.sin(f)], 1).astype(np.float32)
    return {"cst": c, "cos": cos, "sin": sin, "ident": np.eye(P, dtype=np.float32)}


def kernel(**inputs):
    import concourse.bacc as bacc
    from concourse.bass_utils import run_bass_kernel_spmd

    a = {k: np.asarray(v) for k, v in inputs.items()}

    def plain(x):
        return np.ascontiguousarray(x)

    arrays = {k: plain(a[k]) for k in (
        "L0_tok_word_emb L0_tok_pos_emb L0_tok_type_emb L0_tok_gamma L0_tok_beta L0_ffn_Wq L0_ffn_bq L0_ffn_Wdown "
        "L0_ffn_Wup L0_ffn_bup L0_ffn_Wo L0_ffn_bo L0_ffn_Wg L0_ffn_bg L0_ffn_We").split()}
    for k in "L0_attn_wq L0_attn_wk L0_attn_wv L1_attn_Wq L1_attn_Wk L1_attn_Wv L1_attn_Wo".split():
        arrays[k + "T"] = plain(a[k].T)
    arrays["idsT"] = plain(a["x"].T)
    arrays["typesT"] = plain(a["mask_BS_i1_0"].T)
    arrays["gamma1T"] = plain(a["L0_ffn_gamma1"].reshape(KD, P).T)
    arrays["gamma2T"] = plain(a["L0_ffn_gamma2"].reshape(KD, P).T)
    arrays["bdownT"] = plain(a["L0_ffn_bdown"].reshape(LAT, 1))
    arrays["routerT"] = plain(a["L1_ffn_router_w"].T)
    arrays["gateT"] = plain(a["L1_ffn_gate_w"].transpose(0, 2, 1))
    arrays["upT"] = plain(a["L1_ffn_up_w"].transpose(0, 2, 1))
    arrays["downT"] = plain(a["L1_ffn_down_w"].transpose(0, 2, 1))
    arrays.update(constants())

    nc = bacc.Bacc("TRN2", target_bir_lowering=False, num_devices=1)
    dr = {k: nc.dram_tensor(f"in_{k}", v.shape, mybir.dt.from_np(v.dtype), kind="ExternalInput").ap()
          for k, v in arrays.items()}
    dr["out"] = nc.dram_tensor("out", (B * P, D), F32, kind="ExternalOutput").ap()
    build(nc, dr)
    r = run_bass_kernel_spmd(nc, [{f"in_{k}": v for k, v in arrays.items()}], core_ids=[0])
    return r.results[0]["out"].reshape(B, P, D)
```
